# Optimizing a Trainium2 kernel written in Bass

```python
import numpy as np
import jax
import jax.numpy as jnp

def _softmax(x, axis=-1):
    return jax.nn.softmax(x, axis=axis)

def _gelu(x):
    return jax.nn.gelu(x, approximate=True)

def _silu(x):
    return jax.nn.silu(x)

def _sigmoid(x):
    return jax.nn.sigmoid(x)

def _layernorm(x, axis=-1, eps=1e-05):
    m = jnp.mean(x, axis=axis, keepdims=True)
    v = jnp.var(x, axis=axis, keepdims=True)
    return (x - m) / jnp.sqrt(v + eps)

def _scatter_add(tgt, idx, src, axis=0):
    return tgt.at[idx].add(src)

def _segment_sum(src, seg, n):
    return jax.ops.segment_sum(src, seg, n)
kernel_name = 'mk_xattn_seq_d1_seqx_r2_51e4e8'

def setup_inputs(seed: int=0):
    np.random.seed(seed)
    _w = jnp.asarray

    def _rec_inputs():
        import jax
        import jax.numpy as jnp
        _rk = jax.random.key(seed)
        x = -0.0001548 + 1 * jax.random.normal(jax.random.fold_in(_rk, 1), (4, 2048, 640), jnp.float32)
        _lenS = 2048 - jax.random.randint(jax.random.fold_in(_rk, 7), (4,), 0, max(1, 2048 // 4) + 1, jnp.int32)
        _lenS2 = 154 - jax.random.randint(jax.random.fold_in(_rk, 8), (4,), 0, max(1, 154 // 4) + 1, jnp.int32)
        _ctx_768P = jax.random.normal(jax.random.fold_in(_rk, 11), (4, 16, 384), jnp.float32)
        _ctx_768c = jax.random.dirichlet(jax.random.fold_in(_rk, 511), 0.3 * jnp.ones((16,), jnp.float32), (4, 154))
        _ctx_768t = jnp.einsum('bsk,bkd->bsd', _ctx_768c, _ctx_768P)
        _ctx_768t = _ctx_768t * jax.lax.rsqrt(jnp.mean(jnp.square(_ctx_768t)) + 1e-12) * 0.953939
        ctx_768 = 0.00141353 + 0.998943 * (_ctx_768t + 0.3 * jax.random.normal(jax.random.fold_in(_rk, 611), (4, 154, 384), jnp.float32))
        return (x, ctx_768)
    x, ctx_768 = _rec_inputs()

    def _L0_xattn_setup():
        import jax, jax.numpy as jnp
        import numpy as np
        HEADS = 8
        NUM_TOKENS = 4
        CROSS_ATTENTION_DIM = 384

        def _mha(q, k, v, heads=HEADS):
            B, Sq, H = q.shape
            Sk = k.shape[1]
            d = H // heads
            qh = q.reshape(B, Sq, heads, d).transpose(0, 2, 1, 3)
            kh = k.reshape(B, Sk, heads, d).transpose(0, 2, 1, 3)
            vh = v.reshape(B, Sk, heads, d).transpose(0, 2, 1, 3)
            scores = jnp.einsum('bhqd,bhkd->bhqk', qh, kh) * jnp.asarray(d, q.dtype) ** (-0.5)
            probs = jax.nn.softmax(scores, axis=-1)
            out = jnp.einsum('bhqk,bhkd->bhqd', probs, vh)
            return out.transpose(0, 2, 1, 3).reshape(B, Sq, H)
        key = jax.random.key(seed)
        ks = jax.random.split(key, 10)
        B, S, H, CAD, T = (4, 512, 640, CROSS_ATTENTION_DIM, NUM_TOKENS)
        sc = 0.02
        return {'hidden_states': jax.random.normal(ks[0], (B, S, H), jnp.float32), 'encoder_hidden_states': jax.random.normal(ks[1], (B, 77 + T, CAD), jnp.float32), 'Wq': jax.random.normal(ks[2], (H, H), jnp.float32) * sc, 'Wk': jax.random.normal(ks[3], (CAD, H), jnp.float32) * sc, 'Wv': jax.random.normal(ks[4], (CAD, H), jnp.float32) * sc, 'Wq_ca': jax.random.normal(ks[5], (T, H), jnp.float32) * sc, 'Wk_ca': jax.random.normal(ks[6], (CAD, H), jnp.float32) * sc, 'Wv_ca': jax.random.normal(ks[7], (CAD, H), jnp.float32) * sc, 'Wout': jax.random.normal(ks[8], (H, H), jnp.float32) * sc, 'b_out': jnp.zeros((H,), jnp.float32)}
    _L0_xattn_all = _L0_xattn_setup()
    _L0_xattn_in = {k: v for k, v in _L0_xattn_all.items() if k in ('Wq', 'Wk', 'Wv', 'Wq_ca', 'Wk_ca', 'Wv_ca', 'Wout', 'b_out')}
    del _L0_xattn_all
    return {'x': x, 'ctx_768': ctx_768, 'L0_xattn_Wq': _L0_xattn_in['Wq'], 'L0_xattn_Wk': _L0_xattn_in['Wk'], 'L0_xattn_Wv': _L0_xattn_in['Wv'], 'L0_xattn_Wq_ca': _L0_xattn_in['Wq_ca'], 'L0_xattn_Wk_ca': _L0_xattn_in['Wk_ca'], 'L0_xattn_Wv_ca': _L0_xattn_in['Wv_ca'], 'L0_xattn_Wout': _L0_xattn_in['Wout'], 'L0_xattn_b_out': _L0_xattn_in['b_out']}

def reference(x, ctx_768, L0_xattn_Wq, L0_xattn_Wk, L0_xattn_Wv, L0_xattn_Wq_ca, L0_xattn_Wk_ca, L0_xattn_Wv_ca, L0_xattn_Wout, L0_xattn_b_out):
    import jax
    import jax.numpy as jnp

    def _L0_xattn_ref(hidden_states, encoder_hidden_states, Wq, Wk, Wv, Wq_ca, Wk_ca, Wv_ca, Wout, b_out):
        import jax, jax.numpy as jnp
        import numpy as np
        HEADS = 8
        NUM_TOKENS = 4
        CROSS_ATTENTION_DIM = 384

        def _mha(q, k, v, heads=HEADS):
            B, Sq, H = q.shape
            Sk = k.shape[1]
            d = H // heads
            qh = q.reshape(B, Sq, heads, d).transpose(0, 2, 1, 3)
            kh = k.reshape(B, Sk, heads, d).transpose(0, 2, 1, 3)
            vh = v.reshape(B, Sk, heads, d).transpose(0, 2, 1, 3)
            scores = jnp.einsum('bhqd,bhkd->bhqk', qh, kh) * jnp.asarray(d, q.dtype) ** (-0.5)
            probs = jax.nn.softmax(scores, axis=-1)
            out = jnp.einsum('bhqk,bhkd->bhqd', probs, vh)
            return out.transpose(0, 2, 1, 3).reshape(B, Sq, H)
        residual = hidden_states
        unet_size = residual.shape[1]
        end_pos = encoder_hidden_states.shape[1] - NUM_TOKENS
        enc = encoder_hidden_states[:, :end_pos, :]
        ca = encoder_hidden_states[:, end_pos:, :]
        query = hidden_states @ Wq
        keyt = enc @ Wk
        valt = enc @ Wv
        hs = _mha(query, keyt, valt)
        ca_q1 = jnp.einsum('btc,th->bch', ca, Wq_ca)
        indices = np.linspace(0, CROSS_ATTENTION_DIM - 1, unet_size).astype(np.int64)
        ca_q1 = ca_q1[:, indices, :]
        ca_hs1 = _mha(ca_q1, residual, residual)
        ca_q2 = ca_hs1 @ Wq
        ca_k2 = ca @ Wk_ca
        ca_v2 = ca @ Wv_ca
        ca_hs2 = _mha(ca_q2, ca_k2, ca_v2)
        out = hs + ca_hs2
        out = out @ Wout + b_out
        out = out + residual
        return out
    x = _L0_xattn_ref(x, ctx_768, L0_xattn_Wq, L0_xattn_Wk, L0_xattn_Wv, L0_xattn_Wq_ca, L0_xattn_Wk_ca, L0_xattn_Wv_ca, L0_xattn_Wout, L0_xattn_b_out)
    return x

_drawn_inputs = setup_inputs


def setup_inputs(seed=0):
    import zlib

    import numpy as np

    out = dict(_drawn_inputs(seed))
    spreads = {'L0_xattn_b_out': (0.0, 0.1)}
    factors = {'L0_xattn_Wq': 8.0, 'L0_xattn_Wk': 8.0, 'L0_xattn_Wq_ca': 8.0, 'L0_xattn_Wk_ca': 8.0}
    for name, (base, spread) in spreads.items():
        noise = np.random.default_rng([zlib.crc32(name.encode()), seed]).standard_normal(out[name].shape)
        drawn = base * np.exp(spread * noise) if base else spread * noise
        out[name] = jnp.asarray(drawn.astype(out[name].dtype))
    for name, factor in factors.items():
        out[name] = (out[name] * factor).astype(out[name].dtype)
    return out
```

```python
from contextlib import ExitStack

import numpy as np

import concourse.bass as bass
from concourse import mybir

F32 = mybir.dt.float32
F32R = mybir.dt.float32r
ACT = mybir.ActivationFunctionType
ALU = mybir.AluOpType
AX_X = mybir.AxisListType.X

B, S, HID = 4, 2048, 640
HEADS, DH = 8, 80
CAD, TOK, CTX = 384, 4, 154
KEYS = CTX - TOK
SCALE = float(DH) ** -0.5

P = 128
KT = HID // P
CT = CAD // P
CHUNK = 512
CHUNKS = S // CHUNK
ST = CHUNK // P
NST = S // P
VW = DH + 1
REM = KEYS - P
GRP = 4
HT = HEADS * TOK
HALF = HID // 2
BH = B * HT

ROW_OF = np.linspace(0, CAD - 1, S).astype(np.int64)
WIN0 = [int(ROW_OF[CHUNK * i]) for i in range(CHUNKS)]
WIN = max(int(ROW_OF[CHUNK * i + CHUNK - 1]) - WIN0[i] + 1 for i in range(CHUNKS))

TILE_HEADS = [[h for h in range(HEADS) if h * DH < (j + 1) * P and (h + 1) * DH > j * P] for j in range(KT)]
PAIRS = [(j, h) for j in range(KT) for h in TILE_HEADS[j]]
PAIR_AT = {jh: n for n, jh in enumerate(PAIRS)}
BANK_HEADS = [[0, 1, 2], [3, 4, 5], [6, 7]]


def score_runs():
    runs = []
    for bank, heads in enumerate(BANK_HEADS):
        for j in range(KT):
            own = [h for h in TILE_HEADS[j] if h in heads]
            if own:
                runs.append((bank, j, own[0], len(own)))
    return runs


RUNS = score_runs()

T_ORDER = [("x", 0, 0), ("x", 1, 1), ("x", 2, 0), ("x", 3, 1), ("x", 4, 0), ("gather", 0, 1)]
for _t in range(ST):
    if _t:
        T_ORDER += [("o", _t - 1, 0), ("o", _t - 1, 1)]
    T_ORDER += [("p", 3 * _t, 0), ("p", 3 * _t + 1, 1), ("p", 3 * _t + 2, 0)]
T_ORDER += [("o", ST - 1, 0), ("o", ST - 1, 1)]
T_USE, T_TOTAL, T_FREED, T_FREED_TOTAL = {}, [0, 0], {}, [0, 0]
for _name, _n, _bank in T_ORDER:
    T_USE[(_name, _n, _bank)] = T_TOTAL[_bank]
    T_FREED[(_name, _n, _bank)] = T_FREED_TOTAL[_bank]
    T_TOTAL[_bank] += 1
    T_FREED_TOTAL[_bank] += _name != "o"
G_ORDER = [("x", 0, 0), ("x", 1, 1), ("x", 2, 0), ("x", 3, 1), ("x", 4, 0)]
G_USE, G_TOTAL = {}, [0, 0]
for _name, _n, _bank in G_ORDER:
    G_USE[(_name, _n, _bank)] = G_TOTAL[_bank]
    G_TOTAL[_bank] += 1


def constants():
    ident = np.eye(P, dtype=np.float32)
    head_of = np.zeros((P, KT, HEADS), np.float32)
    for j in range(KT):
        for p in range(P):
            head_of[p, j, (j * P + p) // DH] = 1
    block_of = np.zeros((3 * HT, HEADS), np.float32)
    for p in range(3 * HT):
        block_of[p, (p % HT) // TOK] = 1
    pick = np.zeros((CHUNKS, WIN, CHUNK), np.float32)
    for s in range(S):
        pick[s // CHUNK, ROW_OF[s] - WIN0[s // CHUNK], s % CHUNK] = 1
    rem_of = np.zeros((GRP * REM, GRP), np.float32)
    for p in range(GRP * REM):
        rem_of[p, p // REM] = 1
    last_row = np.zeros((VW, 1), np.float32)
    last_row[DH] = 1
    hi_lo = np.eye(2, dtype=np.float32)
    spread = np.tile(np.eye(TOK, dtype=np.float32), (1, 3 * HEADS))
    return {"spread": spread, "ident": ident, "head_of": head_of, "block_of": block_of, "pick": pick, "rem_of": rem_of,
            "last_row": last_row, "hi_lo": hi_lo}


class Steps:

    def __init__(self, eng, sem, rounds, per_round):
        self.eng, self.sem, self.base, self.per_round, self.n = eng, sem, rounds * per_round, per_round, 0

    def done(self, instruction):
        instruction.then_inc(self.sem, 1)
        self.n += 1
        self.eng.wait_ge(self.sem, self.base + self.n)

    def close(self):
        assert self.n == self.per_round, (self.n, self.per_round)


def cross_attention(nc, x, ctx, Wq, Wk, Wv, Wq_ca, Wk_ca, Wv_ca, Wout, b_out,
                    c_ident, c_head_of, c_block_of, c_pick, c_rem_of, c_last_row, c_hi_lo, c_spread, out):
    with ExitStack() as stack:
        def sb(name, shape, dt=F32):
            return stack.enter_context(nc.sbuf_tensor(name, shape, dt))

        def sem(name):
            return stack.enter_context(nc.semaphore(name))

        ident = sb("ident", [P, P])
        head_of = sb("head_of", [P, KT, HEADS])
        block_of = sb("block_of", [3 * HT, HEADS])
        rem_of = sb("rem_of", [GRP * REM, GRP])
        last_row = sb("last_row", [VW, 1])
        spread = sb("spread", [TOK, 3 * HT])
        hi_lo = sb("hi_lo", [P, 2])
        wq_h, wq_l = sb("wq_h", [P, KT, HID], F32R), sb("wq_l", [P, KT, HID], F32R)
        wo_h, wo_l = sb("wo_h", [P, KT, HID], F32R), sb("wo_l", [P, KT, HID], F32R)
        wg_h, wg_l = sb("wg_h", [P, KT, 3 * HT], F32R), sb("wg_l", [P, KT, 3 * HT], F32R)
        m2 = sb("m2", [VW, HEADS, B, HT + 1])
        vw2 = sb("vw2", [3 * HT + 2, B, HID], F32R)
        xc = sb("xc", [P, 2 * ST, HID])
        xt_h, xt_l = sb("xt_h", [P, KT, CHUNK], F32R), sb("xt_l", [P, KT, CHUNK], F32R)
        cawork = sb("cawork", [P, 2 * NST * VW + 4 * CAD])
        xh = cawork[:, 0:2 * NST * VW].rearrange("p (k s v) -> p k s v", k=2, s=NST)
        caw = cawork[:, 2 * NST * VW:].rearrange("p (k c) -> p k c", k=4)
        wk = cawork[:, 0:CT * HID].rearrange("p (k n) -> p k n", k=CT)
        wv = cawork[:, CT * HID:2 * CT * HID].rearrange("p (k n) -> p k n", k=CT)
        g = sb("g", [3 * HT + 1, S], F32R)
        ca_rows4 = sb("ca_rows4", [TOK, CAD])
        ca_all = sb("ca_all", [3 * HT, CAD], F32R)
        ca_head = sb("ca_head", [3 * HT + 1, 2, CAD], F32R)
        hsu = sb("hsu", [P, 2, CAD])
        ctx_in = hsu
        enc_t = sb("enc_t", [P, CT, KEYS])
        unit_max = sb("unit_max", [P, 2, 2 * CT])
        row_max = sb("row_max", [P, 2, CT])
        z_rec = sb("z_rec", [WIN, CHUNKS])
        z_norm = sb("z_norm", [WIN, CHUNKS, HT])
        s2 = sb("s2", [WIN, CHUNKS, HT])
        s2_max = sb("s2_max", [WIN, CHUNKS * HEADS])
        p2 = sb("p2", [WIN, CHUNKS, HT])
        p2_rep = sb("p2_rep", [WIN, CHUNKS, 3, HT])
        p2_chunk = sb("p2_chunk", [WIN, 3 * HT])
        pick = sb("pick", [WIN, CHUNK])
        p2_rows = sb("p2_rows", [3 * HT + 2, CHUNK], F32R)
        keys_bd = sb("keys_bd", [P, len(PAIRS), KEYS])
        v_main = sb("v_main", [P, HEADS, VW])
        v_rem = sb("v_rem", [GRP * REM, 2, GRP, VW])
        v_tail = sb("v_tail", [REM, HID])
        work = sb("work", [P, KT * HID])
        qt = work[:, 0:KT * CHUNK].rearrange("p (j s) -> p j s", j=KT)
        o_norm = work[:, KT * CHUNK:KT * CHUNK + HID]
        probs = sb("probs", [P, HEADS, KEYS])
        probs_rem = sb("probs_rem", [P, HEADS, REM])
        probs_t = sb("probs_t", [P, HEADS + 2, P])
        neg_max = sb("neg_max", [P, 2, HEADS])
        o_rec = sb("o_rec", [P, HEADS])
        ot_h, ot_l = sb("ot_h", [P, HID], F32R), sb("ot_l", [P, HID], F32R)
        o_tile = sb("o_tile", [P, 2, HID])
        stage_w = xc[:, 0:KT, :]
        v2_bd = xc[:, KT:KT + CT, :].rearrange("p a b -> p (a b)").rearrange("p (j b n) -> p j b n", j=KT, b=B)
        wq_t = work[:, :].rearrange("p (j n) -> p j n", j=KT)
        k2_bd = probs_t[:, 0:KT, :]
        wqca_in, bias_in, ca_rows = o_tile[0:TOK, 0, :], o_tile[3 * HT:3 * HT + 2, 0, :], o_tile[0:B * TOK, 1, 0:CAD]
        bias_tmp = o_tile[3 * HT:3 * HT + 2, 1, :]
        small_t = sb("small_t", [P, CT * B * TOK + KT * TOK])
        ca_t = small_t[:, 0:CT * B * TOK].rearrange("p (k n) -> p k n", k=CT)
        wqca_t = small_t[:, CT * B * TOK:].rearrange("p (k n) -> p k n", k=KT)
        kv2_t = sb("kv2_t", [P, 2, KT, B * TOK])
        wg_full = probs[:, 0:2, :].rearrange("p a b -> p (a b)")[:, 0:KT * HT].rearrange("p (k n) -> p k n", k=KT)

        ps_t = stack.enter_context(nc.psum_tensor("ps_t", [P, 2, 512], F32))
        ps_s = stack.enter_context(nc.psum_tensor("ps_s", [P, 3, 512], F32))
        ps_w = stack.enter_context(nc.psum_tensor("ps_w", [P, 3, 512], F32))
        ps_t_flat = ps_t[:, :, :].rearrange("p a b -> p (a b)")
        ps_s_flat = ps_s[:, :, :].rearrange("p a b -> p (a b)")
        ps_w_flat = ps_w[:, :, :].rearrange("p a b -> p (a b)")

        su_in, su_wout_in, su_pe, su_dve = sem("su_in"), sem("su_wout_in"), sem("su_pe"), sem("su_dve")
        dve_setup, dve_batch, dve_head, dve_p2, dve_tile = (
            sem("dve_setup"), sem("dve_batch"), sem("dve_head"), sem("dve_p2"), sem("dve_tile"))
        kv_in, enc_full, enc_ready, kv_full, keys_ready, vals_ready, v_rem_in = (
            sem("kv_in"), sem("enc_full"), sem("enc_ready"), sem("kv_full"), sem("keys_ready"),
            sem("vals_ready"), sem("v_rem_in"))
        ones_set = sem("ones_set")
        xc_in = [sem("xc_in0"), sem("xc_in1")]
        gt_full, gt_free = [sem("gt_full0"), sem("gt_full1")], [sem("gt_free0"), sem("gt_free1")]
        gx_high, gx_used, g_full, g_high, g_ready = (
            sem("gx_high"), sem("gx_used"), sem("g_full"), sem("g_high"), sem("g_ready"))
        xh_in = [sem("xh_in0"), sem("xh_in1")]
        head_set, max_full, max_free, rmax_ready, rmax_t, head_ready = (
            sem("head_set"), sem("max_full"), sem("max_free"), sem("rmax_ready"), sem("rmax_t"), sem("head_ready"))
        sc_full, w_ready, w_used, hsu_ready, z_full, z_free = (
            sem("sc_full"), sem("w_ready"), sem("w_used"), sem("hsu_ready"), sem("z_full"),
            sem("z_free"))
        z_rec_ready, s2_added = sem("z_rec_ready"), sem("s2_added")
        s2_ready, e2_ready, p2_ready = sem("s2_ready"), sem("e2_ready"), sem("p2_ready")
        pick_in, p2c_ready = sem("pick_in"), sem("p2c_ready")
        t_full, t_free = [sem("t_full0"), sem("t_full1")], [sem("t_free0"), sem("t_free1")]
        x_high, q_full, q_ready_act, q_ready_dve = sem("x_high"), sem("q_full"), sem("q_ready_act"), sem("q_ready_dve")
        s_full, nmax_ready, p_ready, rem_ready = sem("s_full"), sem("nmax_ready"), sem("p_ready"), sem("rem_ready")
        ov_full, on_ready, ot_high, ot_low, y_full, ya_ready, y_ready = (
            sem("ov_full"), sem("on_ready"), sem("ot_high"), sem("ot_low"), sem("y_full"),
            sem("ya_ready"), sem("y_ready"))
        stored = [sem("stored0"), sem("stored1")]

        x_rows = x.rearrange("b (c t p) n -> (b c) p t n", t=ST, p=P)
        x_heads = x.rearrange("b (s p) n -> b p s n", p=P)
        out_rows = out.rearrange("b (n p) h -> (b n) p h", p=P)
        SETUP_LOADS = 17
        KV_LOADS = 5

        block = stack.enter_context(nc.Block())

        @block.sync
        def _(sp):
            for dst, src in (
                (ident[:, :], c_ident), (head_of[:, :, :], c_head_of), (block_of[:, :], c_block_of),
                (rem_of[:, :], c_rem_of), (last_row[:, :], c_last_row),
                (hi_lo[3 * HT:3 * HT + 2, :], c_hi_lo), (spread[:, :], c_spread),
                (stage_w, Wq.rearrange("(k p) n -> p k n", p=P)),
                (wk, Wk_ca.rearrange("(k p) n -> p k n", p=P)),
                (wv, Wv_ca.rearrange("(k p) n -> p k n", p=P)),
                (wqca_in, Wq_ca),
                (bias_in[0:1, :], b_out.rearrange("(a n) -> a n", a=1)),
            ):
                sp.dma_start(dst, src).then_inc(su_in, 16)
            sp.dma_start(bias_in[1:2, :], b_out.rearrange("(a n) -> a n", a=1)).then_inc(su_in, 16)
            for b in range(B):
                sp.dma_start(o_tile[b * TOK:(b + 1) * TOK, 1, 0:CAD], ctx[b, KEYS:CTX, :]).then_inc(su_in, 16)
            sp.wait_ge(su_dve, 2)
            sp.dma_start(stage_w, Wout.rearrange("(k p) n -> p k n", p=P)).then_inc(su_wout_in, 16)
            sp.wait_ge(su_dve, 6)

            with sp.Fori(0, B) as b:
                sp.wait_ge(s2_ready, b)
                sp.dma_start(wk, Wk.rearrange("(k p) n -> p k n", p=P)).then_inc(kv_in, 16)
                sp.dma_start(wv, Wv.rearrange("(k p) n -> p k n", p=P)).then_inc(kv_in, 16)
                sp.dma_start(ctx_in[:, 0, :], ctx[bass.ds(b, 1), 0:P, :].rearrange("a p n -> p (a n)")).then_inc(kv_in, 16)
                sp.dma_start(ctx_in[0:REM, 1, :],
                             ctx[bass.ds(b, 1), P:KEYS, :].rearrange("a p n -> p (a n)")).then_inc(kv_in, 16)
                sp.dma_start(ca_rows4[:, :],
                             ctx[bass.ds(b, 1), KEYS:CTX, :].rearrange("a p n -> p (a n)")).then_inc(kv_in, 16)

                def load_x(i, k):
                    sp.dma_start(xc[:, k * ST:(k + 1) * ST, :],
                                 x_rows[bass.ds(b * CHUNKS + i, 1)].rearrange("a p t n -> p (a t) n")).then_inc(xc_in[k], 16)

                def load_head(h, k):
                    sp.dma_start(xh[:, k, :, 0:DH],
                                 x_heads[bass.ds(b, 1), :, :, bass.ds(h * DH, DH)].rearrange("a p s d -> p (a s) d")).then_inc(xh_in[k], 16)

                sp.wait_ge(y_ready, b * NST)
                load_x(0, 0)
                load_x(1, 1)
                for i in range(2, CHUNKS):
                    sp.wait_ge(gt_full[0], (b * CHUNKS + i - 1) * G_TOTAL[0])
                    load_x(i, i % 2)
                sp.wait_ge(vals_ready, b + 1)
                for q in range(GRP):
                    sp.dma_start(v_rem[q * REM:(q + 1) * REM, :, q, 0:DH],
                                 v_tail[:, :].rearrange("p (r q d) -> p r q d", r=2, q=GRP)[:, :, q, :]).then_inc(v_rem_in, 16)
                sp.wait_ge(ones_set, b + 1)
                load_head(0, 0)
                load_head(1, 1)
                for i in range(2):
                    sp.wait_ge(gt_full[0], (b * CHUNKS + i + 3) * G_TOTAL[0])
                    load_x(i, i)
                with sp.Fori(1, HEADS // 2) as hp:
                    for k in range(2):
                        sp.wait_ge(w_used, (b * HEADS + hp * 2 + k - 1) * NST + 4)
                        load_head(hp * 2 + k, k)
                for i in range(CHUNKS):
                    n = b * CHUNKS + i
                    sp.wait_ge(t_free[1], n * T_FREED_TOTAL[1])
                    sp.dma_start(pick[:, :], c_pick[i]).then_inc(pick_in, 16)
                    for t in range(ST):
                        sp.wait_ge(y_ready, n * ST + t + 1)
                        sp.dma_start(out_rows[bass.ds(n * ST + t, 1)].rearrange("a p n -> p (a n)"),
                                     o_tile[:, t % 2, :]).then_inc(stored[t % 2], 16)
                    if i + 2 < CHUNKS:
                        load_x(i + 2, i % 2)
            for k in range(2):
                sp.wait_ge(stored[k], 16 * B * NST // 2)

        def t_turn(n, use):
            return n * T_TOTAL[use[2]] + T_USE[use]

        def t_freed(n, use):
            return n * T_FREED_TOTAL[use[2]] + T_FREED[use]

        def g_turn(n, use):
            return n * G_TOTAL[use[2]] + G_USE[use]

        @block.tensor
        def _(pe):
            def mm(out, lhs, rhs, start, stop):
                return nc.tensor.matmul(out, lhs, rhs, start=start, stop=stop, skip_group_check=True)

            def mm3(out, lhs_h, lhs_l, rhs_h, rhs_l, start, stop):
                mm(out, lhs_h, rhs_h, start, False)
                mm(out, lhs_h, rhs_l, False, False)
                return mm(out, lhs_l, rhs_h, False, stop)

            def turned(out, in_):
                k = in_.shape[0]
                return nc.tensor.transpose(out, in_, ident[0:k, 0:k])

            pe.wait_ge(su_in, 16 * SETUP_LOADS)

            def turn_wq(dst, j):
                for k in range(KT):
                    last = turned(dst[:, k * P:(k + 1) * P], stage_w[:, k, j * P:(j + 1) * P])
                return last

            turn_wq(ps_t_flat, 0)
            turn_wq(ps_s_flat, 1)
            turn_wq(ps_w_flat, 2)
            for c in range(CT):
                turned(ps_s[:, 2, c * B * TOK:(c + 1) * B * TOK], ca_rows[:, c * P:(c + 1) * P])
            for k in range(KT):
                at = CT * B * TOK + k * TOK
                last = turned(ps_s[:, 2, at:at + TOK], wqca_in[:, k * P:(k + 1) * P])
            last.then_inc(su_pe, 1)
            pe.wait_ge(su_dve, 1)
            turn_wq(ps_t_flat, 3)
            turn_wq(ps_s_flat, 4)
            for n, w in enumerate((wk, wv)):
                for j in range(KT):
                    at = (n * KT + j) * B * TOK
                    for c in range(CT):
                        last = mm(ps_w[:, 0, at:at + B * TOK], w[:, c, j * P:(j + 1) * P], ca_t[:, c, :], c == 0, c == CT - 1)
            last.then_inc(su_pe, 1)
            pe.wait_ge(su_dve, 2)
            for h in range(HEADS):
                for j in range(KT):
                    last = mm(ps_s[0:DH, h // 4, h % 4 * BH:(h % 4 + 1) * BH], wq_t[:, j, h * DH:(h + 1) * DH],
                              k2_bd[:, j, :], j == 0, j == KT - 1)
            last.then_inc(su_pe, 1)
            pe.wait_ge(su_wout_in, 16)
            for pair in range(B // 2):
                if pair:
                    pe.wait_ge(su_dve, 4)
                for n, dst in enumerate((ps_t, ps_w)):
                    for half in range(2):
                        for j in range(KT):
                            last = mm(dst[0:3 * HT, half, 0:HALF], v2_bd[:, j, 2 * pair + n, :],
                                      stage_w[:, j, half * HALF:(half + 1) * HALF], j == 0, j == KT - 1)
                last.then_inc(su_pe, 1)
            pe.wait_ge(su_dve, 6)

            def turn_x(turn, full, free, use, k, n):
                _, kt, bank = use
                pe.wait_ge(free[bank], turn(n, use))
                for t in range(ST):
                    last = turned(ps_t[:, bank, t * P:(t + 1) * P], xc[:, k * ST + t, kt * P:(kt + 1) * P])
                last.then_inc(full[bank], 1)

            with pe.Fori(0, B) as b:
                pe.wait_ge(kv_in, 16 * KV_LOADS * (b + 1))
                pe.wait_ge(y_ready, b * NST)
                for c in range(CT):
                    turned(ps_t[:, 0, c * KEYS:c * KEYS + P], ctx_in[:, 0, c * P:(c + 1) * P])
                    last = turned(ps_t[:, 0, c * KEYS + P:(c + 1) * KEYS], ctx_in[0:REM, 1, c * P:(c + 1) * P])
                last.then_inc(enc_full, 1)
                pe.wait_ge(enc_ready, b + 1)
                for j in range(KT):
                    for c in range(CT):
                        mm(ps_s[:, j // 3, j % 3 * KEYS:(j % 3 + 1) * KEYS], wk[:, c, j * P:(j + 1) * P],
                           enc_t[:, c, :], c == 0, c == CT - 1)
                for half in range(2):
                    cols = slice(half * HALF, (half + 1) * HALF)
                    tail = (ps_s[0:REM, 2, 0:HALF], ps_t[0:REM, 1, 0:HALF])[half]
                    for c in range(CT):
                        mm(ps_w[:, half, 0:HALF], enc_t[:, c, 0:P], wv[:, c, cols], c == 0, c == CT - 1)
                    for c in range(CT):
                        mm(tail, enc_t[:, c, P:KEYS], wv[:, c, cols], c == 0, c == CT - 1)
                mm(ps_w[0:3 * HT, 2, 0:CAD], spread[:, :], ca_rows4[:, :], True, True).then_inc(kv_full, 1)

                with pe.Fori(0, CHUNKS // 2) as ip:
                    for k in range(2):
                        n = b * CHUNKS + ip * 2 + k
                        pe.wait_ge(vals_ready, b + 1)
                        pe.wait_ge(xc_in[k], 16 * (b * CHUNKS + ip + 1))
                        turn_x(g_turn, gt_full, gt_free, G_ORDER[0], k, n)
                        turn_x(g_turn, gt_full, gt_free, G_ORDER[1], k, n)
                        for kt in range(KT):
                            use = G_ORDER[kt]
                            pe.wait_ge(gt_free[use[2]], g_turn(n, use) + 1)
                            if kt == 0:
                                pe.wait_ge(g_ready, n)
                            last = mm3(ps_w[0:3 * HT, 0, :], wg_h[:, kt, :], wg_l[:, kt, :], xt_h[:, kt, :],
                                       xt_l[:, kt, :], kt == 0, kt == KT - 1)
                            last.then_inc(gx_used if kt < KT - 1 else g_full, 1)
                            if kt + 2 < KT:
                                turn_x(g_turn, gt_full, gt_free, G_ORDER[kt + 2], k, n)

                def max_unit(h, k, u):
                    c, half = u // 2, u % 2
                    if not (isinstance(h, int) and h == 0 and u < 2):
                        pe.wait_ge(max_free, (b * HEADS + h) * 2 * CT + u - 1)
                    dst = ps_t if half else ps_s
                    for m in range(2):
                        s0 = (half * 2 + m) * 512
                        last = mm(dst[:, m, :], ca_head[0:3 * HT, k, c * P:(c + 1) * P], g[0:3 * HT, s0:s0 + 512], True, True)
                    last.then_inc(max_full, 1)

                def turn_max(h, k):
                    pe.wait_ge(rmax_ready, b * HEADS + h + 1)
                    pe.wait_ge(z_free, b * HEADS + (h - 1 if not isinstance(h, int) or h else 0))
                    for c in range(CT):
                        last = nc.tensor.transpose(ps_w[0:1, 2, c * P:(c + 1) * P], row_max[:, k, c:c + 1], ident[:, :])
                    last.then_inc(rmax_t, 1)

                def weights_sum(h, k):
                    pe.wait_ge(hsu_ready, b * HEADS + h + 1)
                    pe.wait_ge(z_free, b * HEADS + h)
                    for w in range(CHUNKS):
                        last = mm(ps_w[0:WIN, 2, w * (HT + 1):(w + 1) * (HT + 1)], hsu[0:VW, k, WIN0[w]:WIN0[w] + WIN],
                                  m2[:, h, b, :] if isinstance(h, int) and isinstance(b, int) else
                                  m2[:, bass.ds(h, 1), bass.ds(b, 1), :].rearrange("p a c n -> p (a c n)"), True, True)
                    last.then_inc(z_full, 1)

                def scores(h, k, st):
                    mm(ps_w[:, st % 2, 0:CAD], g[:, st * P:(st + 1) * P], ca_head[:, k, :], True, True).then_inc(sc_full, 1)

                def head(h, k, first, last_one):
                    hh = b * HEADS + h
                    pe.wait_ge(head_ready, hh + 1)
                    scores(h, k, 0)
                    scores(h, k, 1)
                    pe.wait_ge(xh_in[k], 16 * (b * (HEADS // 2) + (h // 2 if isinstance(h, int) else hp) + 1))
                    for st in range(NST):
                        pe.wait_ge(w_ready, hh * NST + st + 1)
                        if st == 0:
                            pe.wait_ge(hsu_ready, hh)
                        mm(ps_s[0:VW, 2, 0:CAD], xh[:, k, st, :], caw[:, st % 4, :], st == 0, st == NST - 1).then_inc(w_used, 1)
                        if st + 2 < NST:
                            scores(h, k, st + 2)
                        if st == 3 and not first:
                            weights_sum(h - 1, 1 - k)
                        if not last_one:
                            if st == 0:
                                pe.wait_ge(head_set, hh + 2)
                            if st % 2 == 1 and st < 12:
                                max_unit(h + 1, 1 - k, st // 2)
                            if st == 14:
                                turn_max(h + 1, 1 - k)

                pe.wait_ge(keys_ready, b + 1)
                pe.wait_ge(g_ready, (b + 1) * CHUNKS)
                pe.wait_ge(head_set, b * HEADS + 1)
                for u in range(2 * CT):
                    max_unit(0, 0, u)
                turn_max(0, 0)
                hp = 0
                head(0, 0, True, False)
                head(1, 1, False, False)
                with pe.Fori(1, HEADS // 2 - 1) as hp:
                    head(hp * 2, 0, False, False)
                    head(hp * 2 + 1, 1, False, False)
                head(HEADS - 2, 0, False, False)
                head(HEADS - 1, 1, False, True)
                weights_sum(HEADS - 1, 1)

                with pe.Fori(0, CHUNKS // 2) as ip:
                    for k in range(2):
                        n = b * CHUNKS + ip * 2 + k
                        pe.wait_ge(z_free, (b + 1) * HEADS)
                        pe.wait_ge(v_rem_in, 16 * GRP * (b + 1))
                        pe.wait_ge(xc_in[k], 16 * (b * CHUNKS + 2 + ip + 1))
                        turn_x(t_freed, t_full, t_free, T_ORDER[0], k, n)
                        turn_x(t_freed, t_full, t_free, T_ORDER[1], k, n)
                        pe.wait_ge(y_ready, n * ST)
                        for kt in range(KT):
                            use = T_ORDER[kt]
                            pe.wait_ge(t_free[use[2]], t_freed(n, use) + 1)
                            for j in range(KT):
                                dst = ps_s[:, j, :] if j < 3 else ps_w[:, j - 3, :]
                                cols = slice(j * P, (j + 1) * P)
                                last = mm3(dst, wq_h[:, kt, cols], wq_l[:, kt, cols], xt_h[:, kt, :], xt_l[:, kt, :],
                                           kt == 0, kt == KT - 1)
                                if kt == KT - 1:
                                    last.then_inc(q_full, 1)
                            if kt + 2 < KT:
                                turn_x(t_freed, t_full, t_free, T_ORDER[kt + 2], k, n)
                        pe.wait_ge(pick_in, 16 * (n + 1))
                        pe.wait_ge(p2c_ready, n + 1)
                        use = ("gather", 0, 1)
                        pe.wait_ge(t_free[1], t_freed(n, use))
                        mm(ps_t[0:3 * HT, 1, :], p2_chunk[:, :], pick[:, :], True, True).then_inc(t_full[1], 1)

                        def turn_o(t):
                            pe.wait_ge(on_ready, n * ST + t + 1)
                            for j in range(KT):
                                bank = 0 if j < 4 else 1
                                if j in (0, 4):
                                    pe.wait_ge(t_free[bank], t_freed(n, ("o", t, bank)))
                                last = turned(ps_t_flat[:, j * P:(j + 1) * P], o_norm[:, j * P:(j + 1) * P])
                                if j in (3, 4):
                                    last.then_inc(t_full[bank], 1)

                        def project(t):
                            pe.wait_ge(ot_low, n * ST + t + 1)
                            if t == 0:
                                pe.wait_ge(t_free[1], t_freed(n, ("gather", 0, 1)) + 1)
                            for half in range(2):
                                cols = slice(half * HALF, (half + 1) * HALF)
                                if half == 1:
                                    pe.wait_ge(y_ready, n * ST + t)
                                for kt in range(KT):
                                    rows = slice(kt * P, (kt + 1) * P)
                                    mm3(ps_w[:, half, 0:HALF], ot_h[:, rows], ot_l[:, rows], wo_h[:, kt, cols],
                                        wo_l[:, kt, cols], kt == 0, False)
                                mm(ps_w[:, half, 0:HALF], p2_rows[:, t * P:(t + 1) * P],
                                   vw2[:, bass.ds(b, 1), cols].rearrange("p a n -> p (a n)"), False, True).then_inc(y_full, 1)

                        pe.wait_ge(q_ready_act, 3 * (n + 1))
                        pe.wait_ge(q_ready_dve, 2 * (n + 1))
                        for t in range(ST):
                            seen = None
                            for bank, j, h0, hs in RUNS:
                                if bank == 1 and seen == 0 and t:
                                    turn_o(t - 1)
                                c0 = (h0 - BANK_HEADS[bank][0]) * KEYS
                                at = PAIR_AT[(j, h0)]
                                last = mm(ps_s[:, bank, c0:c0 + hs * KEYS], qt[:, j, t * P:(t + 1) * P],
                                          keys_bd[:, at:at + hs, :].rearrange("p h k -> p (h k)"), bank != seen,
                                          (bank, j) == (RUNS[-1][0], RUNS[-1][1]))
                                seen = bank
                            last.then_inc(s_full, 1)
                            if t:
                                project(t - 1)
                            pe.wait_ge(p_ready, n * ST + t + 1)
                            for part in range(3):
                                use = ("p", 3 * t + part, part % 2)
                                pe.wait_ge(t_free[part % 2], t_freed(n, use))
                                if part < 2:
                                    for q in range(GRP):
                                        last = turned(ps_t[:, part, q * P:(q + 1) * P], probs[:, GRP * part + q, 0:P])
                                else:
                                    pe.wait_ge(rem_ready, n * ST + t + 1)
                                    for r in range(2):
                                        last = turned(ps_t[0:GRP * REM, 0, r * P:(r + 1) * P],
                                                      probs_rem[:, GRP * r:GRP * (r + 1), :].rearrange("p q k -> p (q k)"))
                                last.then_inc(t_full[part % 2], 1)
                            banks = (2, 0)
                            for r in range(2):
                                use = ("p", 3 * t + r, r)
                                pe.wait_ge(t_free[r], t_freed(n, use) + 1)
                                if r == 1:
                                    pe.wait_ge(ya_ready, n * ST + t)
                                for q in range(GRP):
                                    h = GRP * r + q
                                    mm(ps_w[:, banks[r], q * VW:(q + 1) * VW], probs_t[:, h, :], v_main[:, h, :], q == 0, False)
                            pe.wait_ge(t_free[0], t_freed(n, ("p", 3 * t + 2, 0)) + 1)
                            for r in range(2):
                                mm(ps_w[:, banks[r], 0:GRP * VW], probs_t[0:GRP * REM, HEADS + r, :],
                                   v_rem[:, r, :, :].rearrange("p q v -> p (q v)"), False, True).then_inc(ov_full, 1)
                        turn_o(ST - 1)
                        project(ST - 1)

        @block.scalar
        def _(act):
            copy, exp = ACT.Copy, ACT.Exp
            act.wait_ge(su_dve, 6)
            with act.Fori(0, B) as b:
                act.wait_ge(enc_full, b + 1)
                nc.scalar.activation(enc_t[:, :, :].rearrange("p c k -> p (c k)"), ps_t[:, 0, 0:CT * KEYS], copy).then_inc(enc_ready, 1)
                act.wait_ge(kv_full, b + 1)
                for half in range(2):
                    nc.scalar.activation(v_main[:, half * GRP:(half + 1) * GRP, 0:DH],
                                         ps_w[:, half, 0:HALF].rearrange("p (h d) -> p h d", h=GRP), copy)
                    tail = (ps_s[0:REM, 2, 0:HALF], ps_t[0:REM, 1, 0:HALF])[half]
                    last = nc.scalar.activation(v_tail[:, half * HALF:(half + 1) * HALF], tail, copy)
                last.then_inc(vals_ready, 1)
                with act.Fori(0, CHUNKS // 2) as ip:
                    for k in range(2):
                        n = b * CHUNKS + ip * 2 + k
                        for use in G_ORDER:
                            _, kt, bank = use
                            act.wait_ge(gt_full[bank], g_turn(n, use) + 1)
                            if kt < KT - 1:
                                act.wait_ge(gx_used, n * (KT - 1) + kt + 1)
                            else:
                                act.wait_ge(g_full, n)
                            nc.scalar.activation(xt_h[:, kt, :], ps_t[:, bank, :], copy).then_inc(gx_high, 1)

                def head(h, k):
                    hh = b * HEADS + h
                    for st in range(NST):
                        act.wait_ge(sc_full, hh * NST + st + 1)
                        act.wait_ge(w_used, hh * NST + st + 1)
                        nc.scalar.activation(caw[:, st % 4, :], ps_w[:, st % 2, 0:CAD], exp, scale=SCALE).then_inc(w_ready, 1)
                    act.wait_ge(w_used, (hh + 1) * NST + 4)
                    nc.scalar.activation(hsu[0:VW, k, :], ps_s[0:VW, 2, 0:CAD], copy).then_inc(hsu_ready, 1)

                with act.Fori(0, HEADS // 2) as hp:
                    head(hp * 2, 0)
                    head(hp * 2 + 1, 1)
                act.wait_ge(s2_ready, b + 1)
                nc.scalar.activation(p2[:, :, :], s2[:, :, :], exp, scale=SCALE).then_inc(e2_ready, 1)

                with act.Fori(0, CHUNKS // 2) as ip:
                    for k in range(2):
                        n = b * CHUNKS + ip * 2 + k
                        act.wait_ge(q_full, KT * n)
                        for kt in range(KT):
                            use = T_ORDER[kt]
                            act.wait_ge(t_full[use[2]], t_turn(n, use) + 1)
                            nc.scalar.activation(xt_h[:, kt, :], ps_t[:, use[2], :], copy).then_inc(x_high, 1)
                        for j in (0, 2, 4):
                            act.wait_ge(q_full, KT * n + j + 1)
                            src = ps_s[:, j, :] if j < 3 else ps_w[:, j - 3, :]
                            nc.scalar.activation(qt[:, j, :], src, copy).then_inc(q_ready_act, 1)

                        def high_o(t):
                            for bank in range(2):
                                act.wait_ge(t_full[bank], t_turn(n, ("o", t, bank)) + 1)
                            nc.scalar.activation(ot_h[:, :], ps_t_flat[:, 0:HID], copy).then_inc(ot_high, 1)

                        for t in range(ST):
                            if t:
                                high_o(t - 1)
                            act.wait_ge(nmax_ready, n * ST + t + 1)
                            for h in range(HEADS):
                                bank, c = h // 3, h % 3
                                last = nc.scalar.activation(probs[:, h, :], ps_s[:, bank, c * KEYS:(c + 1) * KEYS], exp,
                                                            bias=neg_max[:, t % 2, h:h + 1], scale=SCALE)
                            last.then_inc(p_ready, 1)
                            act.wait_ge(t_full[0], t_turn(n, ("p", 3 * t, 0)) + 1)
                            nc.scalar.activation(probs_t[:, 0:GRP, :],
                                                 ps_t[:, 0, :].rearrange("p (r s) -> p r s", r=GRP), copy).then_inc(t_free[0], 1)
                            act.wait_ge(t_full[0], t_turn(n, ("p", 3 * t + 2, 0)) + 1)
                            nc.scalar.activation(probs_t[0:GRP * REM, HEADS:HEADS + 2, :],
                                                 ps_t[0:GRP * REM, 0, 0:2 * P].rearrange("p (r s) -> p r s", r=2), copy).then_inc(t_free[0], 1)
                        high_o(ST - 1)

        @block.vector
        def _(dve):
            v = nc.vector
            dve.wait_ge(su_in, 16 * SETUP_LOADS)
            steps = Steps(dve, dve_setup, 0, 0)
            v.memset(g[3 * HT:3 * HT + 1, :].bitcast(F32), 1.0).then_inc(gx_used, KT - 1)
            v.memset(p2_rows[3 * HT:3 * HT + 2, :].bitcast(F32), 1.0).then_inc(w_used, 4)
            v.memset(v_main[:, :, DH:VW], 1.0)
            v.memset(m2[:, :, :, :], 0.0)
            steps.done(v.memset(v_rem[:, :, :, :], 0.0))
            v.tensor_copy(m2[:, :, :, HT:HT + 1], last_row[:, :].unsqueeze(1).unsqueeze(1).broadcast_to([VW, HEADS, B, 1]))
            for r in range(2):
                v.tensor_copy(v_rem[:, r, :, DH], rem_of[:, :])
            steps.done(v.tensor_copy(wq_h[:, :, :], stage_w))
            v.tensor_tensor(wq_l[:, :, :], stage_w, wq_h[:, :, :], ALU.subtract)
            dve.wait_ge(su_pe, 1)
            for j, src in enumerate((ps_t_flat, ps_s_flat, ps_w_flat)):
                v.tensor_copy(wq_t[:, j, :], src[:, 0:HID])
            n = CT * B * TOK + KT * TOK
            steps.done(v.tensor_copy(small_t[:, :], ps_s[:, 2, 0:n]))
            wg_src = wqca_t.unsqueeze(2).broadcast_to([P, KT, HEADS, TOK])
            wg_mask = head_of[:, :, :].unsqueeze(3).broadcast_to([P, KT, HEADS, TOK])
            steps.done(v.tensor_tensor(wg_full.rearrange("p k (h t) -> p k h t", h=HEADS), wg_src, wg_mask, ALU.mult))
            for r in range(3):
                last = v.tensor_copy(wg_h[:, :, r * HT:(r + 1) * HT], wg_full)
            steps.done(last)
            for r in range(3):
                last = v.tensor_tensor(wg_l[:, :, r * HT:(r + 1) * HT], wg_full, wg_h[:, :, 0:HT], ALU.subtract)
            last.then_inc(su_dve, 1)
            dve.wait_ge(su_pe, 2)
            v.tensor_copy(wq_t[:, 3, :], ps_t_flat[:, 0:HID])
            v.tensor_copy(wq_t[:, 4, :], ps_s_flat[:, 0:HID])
            steps.done(v.tensor_copy(kv2_t[:, :, :, :].rearrange("p a j n -> p (a j n)"), ps_w[:, 0, 0:2 * KT * B * TOK]))
            for j in range(KT):
                mask = head_of[:, j, :].unsqueeze(1).unsqueeze(3).broadcast_to([P, B, HEADS, TOK])
                k2, v2 = (kv2_t[:, a, j, :].rearrange("p (b t) -> p b t", b=B).unsqueeze(2).broadcast_to([P, B, HEADS, TOK])
                          for a in range(2))
                v.tensor_tensor(k2_bd[:, j, :].rearrange("p (b h t) -> p b h t", b=B, h=HEADS), k2, mask, ALU.mult)
                for r in range(3):
                    last = v.tensor_tensor(v2_bd[:, j, :, r * HT:(r + 1) * HT].rearrange("p b (h t) -> p b h t", h=HEADS),
                                           v2, mask, ALU.mult)
            last.then_inc(su_dve, 1)
            dve.wait_ge(su_pe, 3)
            for a in range(2):
                last = v.tensor_copy(m2[0:DH, a * 4:(a + 1) * 4, :, 0:HT],
                                     ps_s[0:DH, a, :].rearrange("p (h b n) -> p h b n", h=4, b=B))
            last.then_inc(su_dve, 1)
            dve.wait_ge(su_wout_in, 16)
            steps.done(v.tensor_copy(wo_h[:, :, :], stage_w))
            v.tensor_tensor(wo_l[:, :, :], stage_w, wo_h[:, :, :], ALU.subtract)
            for pair in range(B // 2):
                dve.wait_ge(su_pe, 4 + pair)
                for a, src in enumerate((ps_t, ps_w)):
                    dst = vw2[0:3 * HT, 2 * pair + a, :].rearrange("p (a n) -> p a n", a=2)
                    steps.done(v.tensor_copy(dst, src[0:3 * HT, 0:2, 0:HALF]))
                    low = slice(HT, 2 * HT)
                    last = v.tensor_tensor(vw2[low, 2 * pair + a, :].rearrange("p (a n) -> p a n", a=2),
                                           src[low, 0:2, 0:HALF], vw2[low, 2 * pair + a, :].rearrange("p (a n) -> p a n", a=2),
                                           ALU.subtract)
                last.then_inc(su_dve, 1)
            rows = slice(3 * HT, 3 * HT + 2)
            steps.done(v.tensor_copy(vw2[rows, 0, :], bias_in))
            steps.done(v.tensor_tensor(bias_tmp, bias_in, vw2[rows, 0, :], ALU.subtract))
            steps.done(v.tensor_scalar(bias_tmp, bias_tmp, hi_lo[rows, 1:2], None, ALU.mult))
            steps.done(v.scalar_tensor_tensor(bias_in, vw2[rows, 0, :], hi_lo[rows, 0:1], bias_tmp, ALU.mult, ALU.add))
            for b in range(B):
                last = v.tensor_copy(vw2[rows, b, :], bias_in)
            last.then_inc(su_dve, 1)

            def low_x(b, n, k, order, turn, high, free):
                for use in order[0:KT]:
                    _, kt, bank = use
                    dve.wait_ge(high, n * KT + kt + 1)
                    v.tensor_tensor(xt_l[:, kt, :], ps_t[:, bank, :], xt_h[:, kt, :], ALU.subtract).then_inc(free[bank], 1)

            with dve.Fori(0, B) as b:
                dve.wait_ge(kv_full, b + 1)
                steps = Steps(dve, dve_batch, b, 1)
                v.memset(xh[:, :, :, DH:VW], 1.0).then_inc(ones_set, 1)
                for at, (j, h) in enumerate(PAIRS):
                    v.tensor_scalar(keys_bd[:, at, :], ps_s[:, j // 3, j % 3 * KEYS:(j % 3 + 1) * KEYS],
                                    head_of[:, j, h:h + 1], None, ALU.mult)
                steps.done(v.tensor_copy(ca_all[:, :], ps_w[0:3 * HT, 2, 0:CAD]))
                steps.close()
                low = slice(HT, 2 * HT)
                v.tensor_tensor(ca_all[low, :], ps_w[low, 2, 0:CAD], ca_all[low, :], ALU.subtract).then_inc(keys_ready, 1)

                with dve.Fori(0, CHUNKS // 2) as ip:
                    for k in range(2):
                        i = ip * 2 + k
                        n = b * CHUNKS + i
                        low_x(b, n, k, G_ORDER, g_turn, gx_high, gt_free)
                        dve.wait_ge(g_full, n + 1)
                        at = bass.ds(i * CHUNK, CHUNK)
                        v.tensor_copy(g[0:3 * HT, at], ps_w[0:3 * HT, 0, :]).then_inc(g_high, 1)
                        dve.wait_ge(g_high, n + 1)
                        low = slice(2 * HT, 3 * HT)
                        v.tensor_tensor(g[low, at], ps_w[low, 0, :], g[low, at], ALU.subtract).then_inc(g_ready, 1)

                def set_head(h, k):
                    v.tensor_scalar(ca_head[0:3 * HT, k, :], ca_all[:, :],
                                    block_of[:, bass.ds(h, 1)] if not isinstance(h, int) else block_of[:, h:h + 1],
                                    None, ALU.mult).then_inc(head_set, 1)

                def maxima(h, k):
                    first = (b * HEADS + h) * 2 * CT
                    for u in range(2 * CT):
                        dve.wait_ge(max_full, first + u + 1)
                        src = ps_t if u % 2 else ps_s
                        v.tensor_reduce(unit_max[:, k, u:u + 1], src[:, 0:2, :], mybir.AxisListType.XY, ALU.max).then_inc(max_free, 1)
                    dve.wait_ge(max_free, first + 2 * CT)
                    v.tensor_reduce(row_max[:, k, :], unit_max[:, k, :].rearrange("p (c a) -> p c a", a=2), AX_X, ALU.max).then_inc(rmax_ready, 1)
                    dve.wait_ge(rmax_t, b * HEADS + h + 1)
                    v.tensor_scalar(ca_head[3 * HT:3 * HT + 1, k, :], ps_w[0:1, 2, 0:CAD], -1.0, None, ALU.mult).then_inc(head_ready, 1)

                def add_head(h):
                    hh = b * HEADS + h
                    dve.wait_ge(z_full, hh + 1)
                    z = ps_w[0:WIN, 2, 0:CHUNKS * (HT + 1)].rearrange("p (w n) -> p w n", w=CHUNKS)
                    v.reciprocal(z_rec[:, :], z[:, :, HT]).then_inc(z_rec_ready, 1)
                    dve.wait_ge(z_rec_ready, hh + 1)
                    first = isinstance(h, int) and h == 0
                    v.tensor_tensor((s2 if first else z_norm)[:, :, :], z[:, :, 0:HT],
                                    z_rec[:, :].unsqueeze(2).broadcast_to([WIN, CHUNKS, HT]), ALU.mult).then_inc(z_free, 1)
                    dve.wait_ge(z_free, hh + 1)
                    if not first:
                        dve.wait_ge(s2_added, b * (HEADS - 1) + h - 1)
                        v.tensor_tensor(s2[:, :, :], s2[:, :, :], z_norm[:, :, :], ALU.add).then_inc(s2_added, 1)

                def head(h, k, first):
                    dve.wait_ge(sc_full, (b * HEADS + h) * NST)
                    set_head(h + 1, 1 - k)
                    if not first:
                        add_head(h - 1)
                    maxima(h + 1, 1 - k)

                set_head(0, 0)
                maxima(0, 0)
                head(0, 0, True)
                head(1, 1, False)
                with dve.Fori(1, HEADS // 2 - 1) as hp:
                    head(hp * 2, 0, False)
                    head(hp * 2 + 1, 1, False)
                head(HEADS - 2, 0, False)
                add_head(HEADS - 2)
                add_head(HEADS - 1)
                dve.wait_ge(s2_added, (b + 1) * (HEADS - 1))
                steps = Steps(dve, dve_p2, b, 4)
                by_head = lambda a: a[:, :, :].rearrange("p w (h t) -> p (w h) t", t=TOK)
                spread_t = s2_max[:, :].unsqueeze(2).broadcast_to([WIN, CHUNKS * HEADS, TOK])
                steps.done(v.tensor_reduce(s2_max[:, :], by_head(s2), AX_X, ALU.max))
                v.tensor_tensor(by_head(s2), by_head(s2), spread_t, ALU.subtract).then_inc(s2_ready, 1)
                dve.wait_ge(e2_ready, b + 1)
                steps.done(v.tensor_reduce(s2_max[:, :], by_head(p2), AX_X, ALU.add))
                steps.done(v.reciprocal(s2_max[:, :], s2_max[:, :]))
                steps.done(v.tensor_tensor(by_head(p2), by_head(p2), spread_t, ALU.mult))
                for r in range(3):
                    last = v.tensor_copy(p2_rep[:, :, r, :], p2[:, :, :])
                last.then_inc(p2_ready, 1)
                steps.close()

                with dve.Fori(0, CHUNKS // 2) as ip:
                    for k in range(2):
                        i = ip * 2 + k
                        n = b * CHUNKS + i
                        dve.wait_ge(p2_ready, b + 1)
                        v.tensor_copy(p2_chunk[:, :], p2_rep[:, bass.ds(i, 1), :, :].rearrange("p a r n -> p (a r n)")).then_inc(p2c_ready, 1)
                        low_x(b, n, k, T_ORDER, t_turn, x_high, t_free)
                        for j in (1, 3):
                            dve.wait_ge(q_full, KT * n + j + 1)
                            src = ps_s[:, j, :] if j < 3 else ps_w[:, j - 3, :]
                            v.tensor_copy(qt[:, j, :], src).then_inc(q_ready_dve, 1)
                        steps = Steps(dve, dve_tile, n, 1 + 3 * ST)
                        dve.wait_ge(t_full[1], t_turn(n, ("gather", 0, 1)) + 1)
                        steps.done(v.tensor_copy(p2_rows[0:3 * HT, :], ps_t[0:3 * HT, 1, :]))
                        low = slice(2 * HT, 3 * HT)
                        v.tensor_tensor(p2_rows[low, :], ps_t[low, 1, :], p2_rows[low, :], ALU.subtract).then_inc(t_free[1], 1)

                        def low_o(t):
                            dve.wait_ge(ot_high, n * ST + t + 1)
                            v.tensor_tensor(ot_l[:, :], ps_t_flat[:, 0:HID], ot_h[:, :], ALU.subtract).then_inc(ot_low, 1)

                        def add_rows(t):
                            dve.wait_ge(stored[t % 2], 16 * (n * 2 + t // 2))
                            for half in range(2):
                                dve.wait_ge(y_full, (n * ST + t) * 2 + half + 1)
                                cols = slice(half * HALF, (half + 1) * HALF)
                                v.tensor_tensor(o_tile[:, t % 2, cols], ps_w[:, half, 0:HALF], xc[:, k * ST + t, cols],
                                                ALU.add).then_inc((ya_ready, y_ready)[half], 1)

                        for t in range(ST):
                            if t:
                                low_o(t - 1)
                            dve.wait_ge(s_full, n * ST + t + 1)
                            v.tensor_reduce(neg_max[:, t % 2, 0:6].rearrange("p (a h) -> p a h", a=2),
                                            ps_s[:, 0:2, 0:3 * KEYS].rearrange("p a (h k) -> p a h k", h=3), AX_X, ALU.max)
                            steps.done(v.tensor_reduce(neg_max[:, t % 2, 6:8], ps_s[:, 2, 0:2 * KEYS].rearrange("p (h k) -> p h k", h=2),
                                                       AX_X, ALU.max))
                            v.tensor_scalar(neg_max[:, t % 2, :], neg_max[:, t % 2, :], -SCALE, None, ALU.mult).then_inc(nmax_ready, 1)
                            if t:
                                add_rows(t - 1)
                            dve.wait_ge(p_ready, n * ST + t + 1)
                            v.tensor_copy(probs_rem[:, :, :], probs[:, :, P:KEYS]).then_inc(rem_ready, 1)
                            dve.wait_ge(t_full[1], t_turn(n, ("p", 3 * t + 1, 1)) + 1)
                            v.tensor_copy(probs_t[:, GRP:HEADS, :], ps_t[:, 1, :].rearrange("p (r s) -> p r s", r=GRP)).then_inc(t_free[1], 1)
                            for r in range(2):
                                dve.wait_ge(ov_full, (n * ST + t) * 2 + r + 1)
                                o = ps_w[:, 2 if r == 0 else 0, 0:GRP * VW].rearrange("p (q v) -> p q v", q=GRP)
                                steps.done(v.reciprocal(o_rec[:, r * GRP:(r + 1) * GRP], o[:, :, DH]))
                                last = v.tensor_tensor(o_norm[:, r * HALF:(r + 1) * HALF].rearrange("p (q d) -> p q d", q=GRP),
                                                       o[:, :, 0:DH],
                                                       o_rec[:, r * GRP:(r + 1) * GRP].unsqueeze(2).broadcast_to([P, GRP, DH]), ALU.mult)
                            last.then_inc(on_ready, 1)
                        low_o(ST - 1)
                        add_rows(ST - 1)
                        steps.close()


_INS = ["x", "ctx_768", "L0_xattn_Wq", "L0_xattn_Wk", "L0_xattn_Wv", "L0_xattn_Wq_ca", "L0_xattn_Wk_ca",
        "L0_xattn_Wv_ca", "L0_xattn_Wout", "L0_xattn_b_out"]
_CONSTS = ["ident", "head_of", "block_of", "pick", "rem_of", "last_row", "hi_lo", "spread"]


def kernel(**inputs):
    import concourse.bacc as _bacc
    from concourse.bass_utils import run_bass_kernel_spmd as _run

    nc = _bacc.Bacc("TRN2", target_bir_lowering=False, num_devices=1)
    consts = constants()
    arrays, args = {}, []
    for name, a in [(n, inputs[n]) for n in _INS] + [(n, consts[n]) for n in _CONSTS]:
        a = np.ascontiguousarray(a)
        arrays[f"in_{name}_dram"] = a
        args.append(nc.dram_tensor(f"in_{name}_dram", a.shape, mybir.dt.from_np(a.dtype), kind="ExternalInput").ap())
    out = nc.dram_tensor("out_dram", (B, S, HID), F32, kind="ExternalOutput").ap()
    cross_attention(nc, *args, out)
    r = _run(nc, [arrays], core_ids=[0])
    return r.results[0]["out_dram"]
```

```python
from contextlib import ExitStack

import numpy as np

import concourse.bass as bass
from concourse import mybir

F32 = mybir.dt.float32
F32R = mybir.dt.float32r
ACT = mybir.ActivationFunctionType
ALU = mybir.AluOpType
AX_X = mybir.AxisListType.X

B, S, HID = 4, 2048, 640
HEADS, DH = 8, 80
CAD, TOK, CTX = 384, 4, 154
KEYS = CTX - TOK
SCALE = float(DH) ** -0.5

P = 128
KT = HID // P
CT = CAD // P
CHUNK = 512
CHUNKS = S // CHUNK
ST = CHUNK // P
NST = S // P
VW = DH + 1
REM = KEYS - P
GRP = 4
HT = HEADS * TOK
HALF = HID // 2
BH = B * HT

ROW_OF = np.linspace(0, CAD - 1, S).astype(np.int64)
WIN0 = [int(ROW_OF[CHUNK * i]) for i in range(CHUNKS)]
WIN = max(int(ROW_OF[CHUNK * i + CHUNK - 1]) - WIN0[i] + 1 for i in range(CHUNKS))

TILE_HEADS = [[h for h in range(HEADS) if h * DH < (j + 1) * P and (h + 1) * DH > j * P] for j in range(KT)]
PAIRS = [(j, h) for j in range(KT) for h in TILE_HEADS[j]]
PAIR_AT = {jh: n for n, jh in enumerate(PAIRS)}
BANK_HEADS = [[0, 1, 2], [3, 4, 5], [6, 7]]


def score_runs():
    runs = []
    for bank, heads in enumerate(BANK_HEADS):
        for j in range(KT):
            own = [h for h in TILE_HEADS[j] if h in heads]
            if own:
                runs.append((bank, j, own[0], len(own)))
    return runs


RUNS = score_runs()

SLOTS = S // P


def turns():
    order = [("x", 0, kt) for kt in range(KT)] + [("q", 0, j) for j in range(KT)] + [("gather", 0)]
    for s in range(SLOTS):
        c, t = divmod(s, ST)
        ahead = c + 1 < CHUNKS
        if t == ST - 1 and ahead:
            order += [("q", c + 1, j) for j in range(KT)]
        order += [("p", s, part) for part in range(3)]
        if ahead:
            order += [("x", c + 1, kt) for kt in X_TURNS[t]]
        if t == 0 and c:
            order.append(("gather", c))
        order += [("o", s, 0), ("o", s, 1)]
    used, copied, use, bank = [0, 0], [0, 0], {}, 1
    for name in order:
        bank = name[2] if name[0] == "o" else 1 - bank
        use[name] = (bank, used[bank], copied[bank])
        used[bank] += 1
        copied[bank] += name[0] != "o"
    return use, used, copied


X_TURNS = [[], [0, 1], [2, 3, 4], []]
T_USE, T_USED, T_COPIED = turns()
T_HIGH = {}
for _use in T_USE:
    if _use[0] in "xq":
        T_HIGH[_use] = len(T_HIGH)
T_HIGHS = len(T_HIGH)
START = 1
G_ORDER = [("x", 0, 0), ("x", 1, 1), ("x", 2, 0), ("x", 3, 1), ("x", 4, 0)]
G_USE, G_TOTAL = {}, [0, 0]
for _name, _n, _bank in G_ORDER:
    G_USE[(_name, _n, _bank)] = G_TOTAL[_bank]
    G_TOTAL[_bank] += 1


def constants():
    ident = np.eye(P, dtype=np.float32)
    head_of = np.zeros((P, KT, HEADS), np.float32)
    for j in range(KT):
        for p in range(P):
            head_of[p, j, (j * P + p) // DH] = 1
    block_of = np.zeros((3 * HT, HEADS), np.float32)
    for p in range(3 * HT):
        block_of[p, (p % HT) // TOK] = 1
    pick = np.zeros((CHUNKS, WIN, CHUNK), np.float32)
    for s in range(S):
        pick[s // CHUNK, ROW_OF[s] - WIN0[s // CHUNK], s % CHUNK] = 1
    rem_of = np.zeros((GRP * REM, GRP), np.float32)
    for p in range(GRP * REM):
        rem_of[p, p // REM] = 1
    last_row = np.zeros((VW, 1), np.float32)
    last_row[DH] = 1
    hi_lo = np.eye(2, dtype=np.float32)
    spread = np.tile(np.eye(TOK, dtype=np.float32), (1, 3 * HEADS))
    return {"spread": spread, "ident": ident, "head_of": head_of, "block_of": block_of, "pick": pick, "rem_of": rem_of,
            "last_row": last_row, "hi_lo": hi_lo}


class Steps:

    def __init__(self, eng, sem, rounds, per_round):
        self.eng, self.sem, self.base, self.per_round, self.n = eng, sem, rounds * per_round, per_round, 0

    def done(self, instruction):
        instruction.then_inc(self.sem, 1)
        self.n += 1
        self.eng.wait_ge(self.sem, self.base + self.n)

    def close(self):
        assert self.n == self.per_round, (self.n, self.per_round)


def cross_attention(nc, x, ctx, Wq, Wk, Wv, Wq_ca, Wk_ca, Wv_ca, Wout, b_out,
                    c_ident, c_head_of, c_block_of, c_pick, c_rem_of, c_last_row, c_hi_lo, c_spread, out):
    with ExitStack() as stack:
        def sb(name, shape, dt=F32):
            return stack.enter_context(nc.sbuf_tensor(name, shape, dt))

        def sem(name):
            return stack.enter_context(nc.semaphore(name))

        ident = sb("ident", [P, P])
        head_of = sb("head_of", [P, KT, HEADS])
        block_of = sb("block_of", [3 * HT, HEADS])
        rem_of = sb("rem_of", [GRP * REM, GRP])
        last_row = sb("last_row", [VW, 1])
        spread = sb("spread", [TOK, 3 * HT])
        hi_lo = sb("hi_lo", [P, 2])
        wq_h, wq_l = sb("wq_h", [P, KT, HID], F32R), sb("wq_l", [P, KT, HID], F32R)
        wo_h, wo_l = sb("wo_h", [P, KT, HID], F32R), sb("wo_l", [P, KT, HID], F32R)
        wg_h, wg_l = sb("wg_h", [P, KT, 3 * HT], F32R), sb("wg_l", [P, KT, 3 * HT], F32R)
        m2 = sb("m2", [VW, HEADS, B, HT + 1])
        vw2_b = sb("vw2_b", [3 * HT + 2, HID], F32R)
        vw2_all = nc.dram_tensor("vw2_all", (3 * HT + 2, B, HID), F32, kind="Internal").ap()
        xc = sb("xc", [P, 2 * ST, HID])
        xt_h, xt_l = sb("xt_h", [P, KT, CHUNK], F32R), sb("xt_l", [P, KT, CHUNK], F32R)
        cawork = sb("cawork", [P, 2 * NST * VW + 4 * CAD])
        xh = cawork[:, 0:2 * NST * VW].rearrange("p (k s v) -> p k s v", k=2, s=NST)
        caw = cawork[:, 2 * NST * VW:].rearrange("p (k c) -> p k c", k=4)
        wk = cawork[:, 0:CT * HID].rearrange("p (k n) -> p k n", k=CT)
        wv = cawork[:, CT * HID:2 * CT * HID].rearrange("p (k n) -> p k n", k=CT)
        ca_rows4 = sb("ca_rows4", [TOK, CAD])
        ca_all = sb("ca_all", [3 * HT, CAD], F32R)
        ca_head = sb("ca_head", [3 * HT + 1, 2, CAD], F32R)
        hsu = sb("hsu", [P, 2, CAD])
        ctx_in = hsu
        enc_t = sb("enc_t", [P, CT, KEYS])
        unit_max = sb("unit_max", [P, 2, 2 * CT])
        row_max = sb("row_max", [P, 2, CT])
        z_rec = sb("z_rec", [WIN, CHUNKS])
        z_norm = sb("z_norm", [WIN, CHUNKS, HT])
        s2 = sb("s2", [WIN, CHUNKS, HT])
        s2_max = sb("s2_max", [WIN, CHUNKS * HEADS])
        p2 = sb("p2", [WIN, CHUNKS, HT])
        p2_rep = sb("p2_rep", [WIN, CHUNKS, 3, HT])
        p2_chunk = sb("p2_chunk", [WIN, 3 * HT])
        pick = sb("pick", [WIN, CHUNK])
        p2_rows = sb("p2_rows", [3 * HT + 2, CHUNK], F32R)
        keys_h, keys_l = sb("keys_h", [P, len(PAIRS), KEYS], F32R), sb("keys_l", [P, len(PAIRS), KEYS], F32R)
        v_main = sb("v_main", [P, HEADS, VW])
        v_rem = sb("v_rem", [GRP * REM, 2, GRP, VW])
        v_tail = sb("v_tail", [REM, HID])
        qt_h, qt_l = sb("qt_h", [P, KT, CHUNK], F32R), sb("qt_l", [P, KT, CHUNK], F32R)
        g = qt_l[0:3 * HT + 1, 0:CHUNKS, :].rearrange("p j s -> p (j s)")
        o_norm = sb("o_norm", [P, HID])
        probs = sb("probs", [P, HEADS, KEYS])
        probs_rem = sb("probs_rem", [P, HEADS, REM])
        probs_t = sb("probs_t", [P, HEADS + 2, P])
        neg_max = sb("neg_max", [P, 2, HEADS])
        o_rec = sb("o_rec", [P, HEADS])
        ot_h, ot_l = sb("ot_h", [P, HID], F32R), sb("ot_l", [P, HID], F32R)
        o_tile = sb("o_tile", [P, 2, HID])
        stage_w = xc[:, 0:KT, :]
        wq_t = [xc[:, KT + j, :] for j in range(3)] + [o_norm[:, :], probs_t[:, 5:10, :].rearrange("p a b -> p (a b)")]
        v2_bd = cawork[:, 0:KT * B * 3 * HT].rearrange("p (j b n) -> p j b n", j=KT, b=B)
        vw2 = xt_h[:, :, :].rearrange("p j s -> p (j s)").rearrange("p (b n) -> p b n", b=B)
        k2_bd = probs_t[:, 0:KT, :]
        wqca_in, bias_in, ca_rows = o_tile[0:TOK, 0, :], o_tile[3 * HT:3 * HT + 2, 0, :], o_tile[0:B * TOK, 1, 0:CAD]
        bias_tmp = o_tile[3 * HT:3 * HT + 2, 1, :]
        small_t = sb("small_t", [P, CT * B * TOK + KT * TOK])
        ca_t = small_t[:, 0:CT * B * TOK].rearrange("p (k n) -> p k n", k=CT)
        wqca_t = small_t[:, CT * B * TOK:].rearrange("p (k n) -> p k n", k=KT)
        kv2_t = sb("kv2_t", [P, 2, KT, B * TOK])
        wg_full = probs[:, 0:2, :].rearrange("p a b -> p (a b)")[:, 0:KT * HT].rearrange("p (k n) -> p k n", k=KT)

        ps_t = stack.enter_context(nc.psum_tensor("ps_t", [P, 2, 512], F32))
        ps_s = stack.enter_context(nc.psum_tensor("ps_s", [P, 3, 512], F32))
        ps_w = stack.enter_context(nc.psum_tensor("ps_w", [P, 3, 512], F32))
        ps_t_flat = ps_t[:, :, :].rearrange("p a b -> p (a b)")
        ps_s_flat = ps_s[:, :, :].rearrange("p a b -> p (a b)")
        ps_w_flat = ps_w[:, :, :].rearrange("p a b -> p (a b)")

        su_in, su_wout_in, su_pe, su_dve = sem("su_in"), sem("su_wout_in"), sem("su_pe"), sem("su_dve")
        dve_setup, dve_batch, dve_head, dve_p2, dve_tile = (
            sem("dve_setup"), sem("dve_batch"), sem("dve_head"), sem("dve_p2"), sem("dve_tile"))
        kv_in, enc_full, enc_ready, kv_full, keys_ready, vals_ready, v_rem_in = (
            sem("kv_in"), sem("enc_full"), sem("enc_ready"), sem("kv_full"), sem("keys_ready"),
            sem("vals_ready"), sem("v_rem_in"))
        ones_set = sem("ones_set")
        xc_in = [sem("xc_in0"), sem("xc_in1")]
        gt_full, gt_free = [sem("gt_full0"), sem("gt_full1")], [sem("gt_free0"), sem("gt_free1")]
        gx_high, gx_used, g_full, g_high, g_ready = (
            sem("gx_high"), sem("gx_used"), sem("g_full"), sem("g_high"), sem("g_ready"))
        xh_in = [sem("xh_in0"), sem("xh_in1")]
        head_set, max_full, max_free, rmax_ready, rmax_t, head_ready = (
            sem("head_set"), sem("max_full"), sem("max_free"), sem("rmax_ready"), sem("rmax_t"), sem("head_ready"))
        sc_full, w_ready, w_used, hsu_ready, z_full, z_free = (
            sem("sc_full"), sem("w_ready"), sem("w_used"), sem("hsu_ready"), sem("z_full"),
            sem("z_free"))
        z_rec_ready, s2_added = sem("z_rec_ready"), sem("s2_added")
        s2_ready, e2_ready, p2_ready = sem("s2_ready"), sem("e2_ready"), sem("p2_ready")
        pick_in, p2c_ready = sem("pick_in"), sem("p2c_ready")
        vw2_out, vw2_in, t_high = sem("vw2_out"), sem("vw2_in"), sem("t_high")
        t_full, t_free = [sem("t_full0"), sem("t_full1")], [sem("t_free0"), sem("t_free1")]
        s_full, nmax_ready, p_ready, rem_ready = sem("s_full"), sem("nmax_ready"), sem("p_ready"), sem("rem_ready")
        ov_full, on_ready, ot_high, ot_low, y_full, ya_ready, y_ready = (
            sem("ov_full"), sem("on_ready"), sem("ot_high"), sem("ot_low"), sem("y_full"),
            sem("ya_ready"), sem("y_ready"))
        stored = [sem("stored0"), sem("stored1")]

        x_rows = x.rearrange("b (c t p) n -> (b c) p t n", t=ST, p=P)
        x_heads = x.rearrange("b (s p) n -> b p s n", p=P)
        out_rows = out.rearrange("b (n p) h -> (b n) p h", p=P)
        SETUP_LOADS = 17
        KV_LOADS = 5

        block = stack.enter_context(nc.Block())

        def bank_of(use):
            return T_USE[use][0]

        def filled(b, use):
            return b * T_USED[T_USE[use][0]] + T_USE[use][1] + 1

        def before(b, use):
            return START + b * T_COPIED[T_USE[use][0]] + T_USE[use][2]

        def copied(b, use):
            return before(b, use) + 1

        def g_turn(n, use):
            return n * G_TOTAL[use[2]] + G_USE[use]

        @block.sync
        def _(sp):
            for dst, src in (
                (ident[:, :], c_ident), (head_of[:, :, :], c_head_of), (block_of[:, :], c_block_of),
                (rem_of[:, :], c_rem_of), (last_row[:, :], c_last_row),
                (hi_lo[3 * HT:3 * HT + 2, :], c_hi_lo), (spread[:, :], c_spread),
                (stage_w, Wq.rearrange("(k p) n -> p k n", p=P)),
                (wk, Wk_ca.rearrange("(k p) n -> p k n", p=P)),
                (wv, Wv_ca.rearrange("(k p) n -> p k n", p=P)),
                (wqca_in, Wq_ca),
                (bias_in[0:1, :], b_out.rearrange("(a n) -> a n", a=1)),
            ):
                sp.dma_start(dst, src).then_inc(su_in, 16)
            sp.dma_start(bias_in[1:2, :], b_out.rearrange("(a n) -> a n", a=1)).then_inc(su_in, 16)
            for b in range(B):
                sp.dma_start(o_tile[b * TOK:(b + 1) * TOK, 1, 0:CAD], ctx[b, KEYS:CTX, :]).then_inc(su_in, 16)
            sp.wait_ge(su_dve, 2)
            sp.dma_start(stage_w, Wout.rearrange("(k p) n -> p k n", p=P)).then_inc(su_wout_in, 16)
            sp.wait_ge(su_dve, 6)
            sp.dma_start(vw2_all, vw2[0:3 * HT + 2, :, :].bitcast(F32)).then_inc(vw2_out, 16)
            sp.wait_ge(vw2_out, 16)

            with sp.Fori(0, B) as b:
                sp.wait_ge(s2_ready, START + b)
                sp.dma_start(wk, Wk.rearrange("(k p) n -> p k n", p=P)).then_inc(kv_in, 16)
                sp.dma_start(wv, Wv.rearrange("(k p) n -> p k n", p=P)).then_inc(kv_in, 16)
                sp.dma_start(ctx_in[:, 0, :], ctx[bass.ds(b, 1), 0:P, :].rearrange("a p n -> p (a n)")).then_inc(kv_in, 16)
                sp.dma_start(ctx_in[0:REM, 1, :],
                             ctx[bass.ds(b, 1), P:KEYS, :].rearrange("a p n -> p (a n)")).then_inc(kv_in, 16)
                sp.dma_start(ca_rows4[:, :],
                             ctx[bass.ds(b, 1), KEYS:CTX, :].rearrange("a p n -> p (a n)")).then_inc(kv_in, 16)

                def load_x(i, k):
                    sp.dma_start(xc[:, k * ST:(k + 1) * ST, :],
                                 x_rows[bass.ds(b * CHUNKS + i, 1)].rearrange("a p t n -> p (a t) n")).then_inc(xc_in[k], 16)

                def load_head(h, k):
                    sp.dma_start(xh[:, k, :, 0:DH],
                                 x_heads[bass.ds(b, 1), :, :, bass.ds(h * DH, DH)].rearrange("a p s d -> p (a s) d")).then_inc(xh_in[k], 16)

                sp.wait_ge(y_ready, START + b * NST)
                load_x(0, 0)
                load_x(1, 1)
                sp.dma_start(vw2_b[:, :].bitcast(F32), vw2_all[:, bass.ds(b, 1), :].rearrange("p a n -> p (a n)")).then_inc(vw2_in, 16)
                for i in range(2, CHUNKS):
                    sp.wait_ge(gt_full[0], (b * CHUNKS + i - 1) * G_TOTAL[0])
                    load_x(i, i % 2)
                sp.wait_ge(vals_ready, b + 1)
                for q in range(GRP):
                    sp.dma_start(v_rem[q * REM:(q + 1) * REM, :, q, 0:DH],
                                 v_tail[:, :].rearrange("p (r q d) -> p r q d", r=2, q=GRP)[:, :, q, :]).then_inc(v_rem_in, 16)
                sp.wait_ge(ones_set, b + 1)
                load_head(0, 0)
                load_head(1, 1)
                for i in range(2):
                    sp.wait_ge(gt_full[0], (b * CHUNKS + i + 3) * G_TOTAL[0])
                    load_x(i, i)
                with sp.Fori(1, HEADS // 2) as hp:
                    for k in range(2):
                        sp.wait_ge(w_used, (b * HEADS + hp * 2 + k - 1) * NST + 4)
                        load_head(hp * 2 + k, k)
                for c in range(CHUNKS):
                    if c:
                        sp.wait_ge(t_full[bank_of(("gather", c - 1))], filled(b, ("gather", c - 1)))
                    sp.dma_start(pick[:, :], c_pick[c]).then_inc(pick_in, 16)
                    if 1 <= c < CHUNKS - 1:
                        sp.wait_ge(y_ready, START + b * SLOTS + c * ST)
                        load_x(c + 1, (c + 1) % 2)

        @block.tensor
        def _(pe):
            def mm(out, lhs, rhs, start, stop):
                return nc.tensor.matmul(out, lhs, rhs, start=start, stop=stop, skip_group_check=True)

            def mm3(out, lhs_h, lhs_l, rhs_h, rhs_l, start, stop):
                mm(out, lhs_h, rhs_h, start, False)
                mm(out, lhs_h, rhs_l, False, False)
                return mm(out, lhs_l, rhs_h, False, stop)

            def turned(out, in_):
                k = in_.shape[0]
                return nc.tensor.transpose(out, in_, ident[0:k, 0:k])

            pe.wait_ge(su_in, 16 * SETUP_LOADS)

            def turn_wq(dst, j):
                for k in range(KT):
                    last = turned(dst[:, k * P:(k + 1) * P], stage_w[:, k, j * P:(j + 1) * P])
                return last

            turn_wq(ps_t_flat, 0)
            turn_wq(ps_s_flat, 1)
            turn_wq(ps_w_flat, 2)
            for c in range(CT):
                turned(ps_s[:, 2, c * B * TOK:(c + 1) * B * TOK], ca_rows[:, c * P:(c + 1) * P])
            for k in range(KT):
                at = CT * B * TOK + k * TOK
                last = turned(ps_s[:, 2, at:at + TOK], wqca_in[:, k * P:(k + 1) * P])
            last.then_inc(su_pe, 1)
            pe.wait_ge(su_dve, 1)
            turn_wq(ps_t_flat, 3)
            turn_wq(ps_s_flat, 4)
            for n, w in enumerate((wk, wv)):
                for j in range(KT):
                    at = (n * KT + j) * B * TOK
                    for c in range(CT):
                        last = mm(ps_w[:, 0, at:at + B * TOK], w[:, c, j * P:(j + 1) * P], ca_t[:, c, :], c == 0, c == CT - 1)
            last.then_inc(su_pe, 1)
            pe.wait_ge(su_dve, 2)
            for h in range(HEADS):
                for j in range(KT):
                    last = mm(ps_s[0:DH, h // 4, h % 4 * BH:(h % 4 + 1) * BH], wq_t[j][:, h * DH:(h + 1) * DH],
                              k2_bd[:, j, :], j == 0, j == KT - 1)
            last.then_inc(su_pe, 1)
            pe.wait_ge(su_wout_in, 16)
            for pair in range(B // 2):
                if pair:
                    pe.wait_ge(su_dve, 4)
                for n, dst in enumerate((ps_t, ps_w)):
                    for half in range(2):
                        for j in range(KT):
                            last = mm(dst[0:3 * HT, half, 0:HALF], v2_bd[:, j, 2 * pair + n, :],
                                      stage_w[:, j, half * HALF:(half + 1) * HALF], j == 0, j == KT - 1)
                last.then_inc(su_pe, 1)
            pe.wait_ge(su_dve, 6)

            def turn_x(k, kt, bank, full):
                for t in range(ST):
                    last = turned(ps_t[:, bank, t * P:(t + 1) * P], xc[:, k * ST + t, kt * P:(kt + 1) * P])
                last.then_inc(full[bank], 1)

            with pe.Fori(0, B) as b:
                pe.wait_ge(kv_in, 16 * KV_LOADS * (b + 1))
                pe.wait_ge(y_ready, START + b * NST)
                for c in range(CT):
                    turned(ps_t[:, 0, c * KEYS:c * KEYS + P], ctx_in[:, 0, c * P:(c + 1) * P])
                    last = turned(ps_t[:, 0, c * KEYS + P:(c + 1) * KEYS], ctx_in[0:REM, 1, c * P:(c + 1) * P])
                last.then_inc(enc_full, 1)
                pe.wait_ge(enc_ready, b + 1)
                for j in range(KT):
                    for c in range(CT):
                        mm(ps_s[:, j // 3, j % 3 * KEYS:(j % 3 + 1) * KEYS], wk[:, c, j * P:(j + 1) * P],
                           enc_t[:, c, :], c == 0, c == CT - 1)
                for half in range(2):
                    cols = slice(half * HALF, (half + 1) * HALF)
                    tail = (ps_s[0:REM, 2, 0:HALF], ps_t[0:REM, 1, 0:HALF])[half]
                    for c in range(CT):
                        mm(ps_w[:, half, 0:HALF], enc_t[:, c, 0:P], wv[:, c, cols], c == 0, c == CT - 1)
                    for c in range(CT):
                        mm(tail, enc_t[:, c, P:KEYS], wv[:, c, cols], c == 0, c == CT - 1)
                mm(ps_w[0:3 * HT, 2, 0:CAD], spread[:, :], ca_rows4[:, :], True, True).then_inc(kv_full, 1)

                with pe.Fori(0, CHUNKS // 2) as ip:
                    for k in range(2):
                        n = b * CHUNKS + ip * 2 + k
                        pe.wait_ge(vals_ready, b + 1)
                        pe.wait_ge(xc_in[k], 16 * (b * CHUNKS + ip + 1))

                        def turn_for_g(use):
                            pe.wait_ge(gt_free[use[2]], START + g_turn(n, use))
                            turn_x(k, use[1], use[2], gt_full)

                        turn_for_g(G_ORDER[0])
                        turn_for_g(G_ORDER[1])
                        for kt in range(KT):
                            use = G_ORDER[kt]
                            pe.wait_ge(gt_free[use[2]], START + g_turn(n, use) + 1)
                            if kt == 0:
                                pe.wait_ge(g_ready, START + n)
                            last = mm3(ps_w[0:3 * HT, 0, :], wg_h[:, kt, :], wg_l[:, kt, :], xt_h[:, kt, :],
                                       xt_l[:, kt, :], kt == 0, kt == KT - 1)
                            last.then_inc(gx_used if kt < KT - 1 else g_full, 1)
                            if kt + 2 < KT:
                                turn_for_g(G_ORDER[kt + 2])

                def max_unit(h, k, u):
                    c, half = u // 2, u % 2
                    if not (isinstance(h, int) and h == 0 and u < 2):
                        pe.wait_ge(max_free, (b * HEADS + h) * 2 * CT + u - 1)
                    dst = ps_t if half else ps_s
                    for m in range(2):
                        s0 = (half * 2 + m) * 512
                        last = mm(dst[:, m, :], ca_head[0:3 * HT, k, c * P:(c + 1) * P], g[0:3 * HT, s0:s0 + 512], True, True)
                    last.then_inc(max_full, 1)

                def turn_max(h, k):
                    pe.wait_ge(rmax_ready, b * HEADS + h + 1)
                    pe.wait_ge(z_free, START + b * HEADS + (h - 1 if not isinstance(h, int) or h else 0))
                    for c in range(CT):
                        last = nc.tensor.transpose(ps_w[0:1, 2, c * P:(c + 1) * P], row_max[:, k, c:c + 1], ident[:, :])
                    last.then_inc(rmax_t, 1)

                def weights_sum(h, k):
                    pe.wait_ge(hsu_ready, START + b * HEADS + h + 1)
                    pe.wait_ge(z_free, START + b * HEADS + h)
                    for w in range(CHUNKS):
                        last = mm(ps_w[0:WIN, 2, w * (HT + 1):(w + 1) * (HT + 1)], hsu[0:VW, k, WIN0[w]:WIN0[w] + WIN],
                                  m2[:, h, b, :] if isinstance(h, int) and isinstance(b, int) else
                                  m2[:, bass.ds(h, 1), bass.ds(b, 1), :].rearrange("p a c n -> p (a c n)"), True, True)
                    last.then_inc(z_full, 1)

                def scores(h, k, st):
                    mm(ps_w[:, st % 2, 0:CAD], g[:, st * P:(st + 1) * P], ca_head[:, k, :], True, True).then_inc(sc_full, 1)

                def head(h, k, first, last_one):
                    hh = b * HEADS + h
                    pe.wait_ge(head_ready, hh + 1)
                    scores(h, k, 0)
                    scores(h, k, 1)
                    pe.wait_ge(xh_in[k], 16 * (b * (HEADS // 2) + (h // 2 if isinstance(h, int) else hp) + 1))
                    for st in range(NST):
                        pe.wait_ge(w_ready, hh * NST + st + 1)
                        if st == 0:
                            pe.wait_ge(hsu_ready, START + hh)
                        mm(ps_s[0:VW, 2, 0:CAD], xh[:, k, st, :], caw[:, st % 4, :], st == 0, st == NST - 1).then_inc(w_used, 1)
                        if st + 2 < NST:
                            scores(h, k, st + 2)
                        if st == 3 and not first:
                            weights_sum(h - 1, 1 - k)
                        if not last_one:
                            if st == 0:
                                pe.wait_ge(head_set, hh + 2)
                            if st % 2 == 1 and st < 12:
                                max_unit(h + 1, 1 - k, st // 2)
                            if st == 14:
                                turn_max(h + 1, 1 - k)

                pe.wait_ge(keys_ready, b + 1)
                pe.wait_ge(g_ready, START + (b + 1) * CHUNKS)
                pe.wait_ge(head_set, b * HEADS + 1)
                for u in range(2 * CT):
                    max_unit(0, 0, u)
                turn_max(0, 0)
                hp = 0
                head(0, 0, True, False)
                head(1, 1, False, False)
                with pe.Fori(1, HEADS // 2 - 1) as hp:
                    head(hp * 2, 0, False, False)
                    head(hp * 2 + 1, 1, False, False)
                head(HEADS - 2, 0, False, False)
                head(HEADS - 1, 1, False, True)
                weights_sum(HEADS - 1, 1)

                pe.wait_ge(z_free, START + (b + 1) * HEADS)
                pe.wait_ge(v_rem_in, 16 * GRP * (b + 1))
                tile0, chunk0 = b * SLOTS, b * CHUNKS

                def turn_for_q(c, kts):
                    if 0 in kts:
                        pe.wait_ge(xc_in[c % 2], 16 * (b * CHUNKS + 2 + c // 2 + 1))
                    for kt in kts:
                        use = ("x", c, kt)
                        pe.wait_ge(t_free[bank_of(use)], before(b, use))
                        turn_x(c % 2, kt, bank_of(use), t_full)

                def queries(c):
                    if c:
                        pe.wait_ge(ot_low, tile0 + c * ST - 1)
                    for j in range(KT):
                        use = ("q", c, j)
                        if j == 0:
                            pe.wait_ge(t_free[bank_of(use)], before(b, use))
                            pe.wait_ge(t_free[1 - bank_of(use)], before(b, ("q", c, 1)))
                        elif j > 1:
                            pe.wait_ge(t_free[bank_of(use)], before(b, use))
                        cols = slice(j * P, (j + 1) * P)
                        for kt in range(KT):
                            last = mm3(ps_t[:, bank_of(use), :], wq_h[:, kt, cols], wq_l[:, kt, cols], xt_h[:, kt, :],
                                       xt_l[:, kt, :], kt == 0, kt == KT - 1)
                        last.then_inc(t_full[bank_of(use)], 1)

                def gather(c):
                    use = ("gather", c)
                    pe.wait_ge(pick_in, 16 * (chunk0 + c + 1))
                    pe.wait_ge(p2c_ready, chunk0 + c + 1)
                    pe.wait_ge(t_free[bank_of(use)], before(b, use))
                    mm(ps_t[0:3 * HT, bank_of(use), :], p2_chunk[:, :], pick[:, :], True, True).then_inc(t_full[bank_of(use)], 1)

                def tile_scores(s):
                    c, t = divmod(s, ST)
                    if s:
                        pe.wait_ge(p_ready, tile0 + s)
                    seen = None
                    for bank, j, h0, hs in RUNS:
                        if t == 0:
                            pe.wait_ge(t_free[bank_of(("q", c, j))], copied(b, ("q", c, j)))
                        c0 = (h0 - BANK_HEADS[bank][0]) * KEYS
                        at = PAIR_AT[(j, h0)]
                        rows = slice(t * P, (t + 1) * P)
                        last = mm3(ps_s[:, bank, c0:c0 + hs * KEYS], qt_h[:, j, rows], qt_l[:, j, rows],
                                   keys_h[:, at:at + hs, :].rearrange("p h k -> p (h k)"),
                                   keys_l[:, at:at + hs, :].rearrange("p h k -> p (h k)"), bank != seen, True)
                        seen = bank
                    last.then_inc(s_full, 1)

                def turn_weights(s):
                    if s:
                        pe.wait_ge(ot_low, tile0 + s)
                    pe.wait_ge(p_ready, tile0 + s + 1)
                    pe.wait_ge(rem_ready, tile0 + s + 1)
                    for part in range(3):
                        use = ("p", s, part)
                        bank = bank_of(use)
                        pe.wait_ge(t_free[bank], before(b, use))
                        if part < 2:
                            for q in range(GRP):
                                last = turned(ps_t[:, bank, q * P:(q + 1) * P], probs[:, GRP * part + q, 0:P])
                        else:
                            for r in range(2):
                                last = turned(ps_t[0:GRP * REM, bank, r * P:(r + 1) * P],
                                              probs_rem[:, GRP * r:GRP * (r + 1), :].rearrange("p q k -> p (q k)"))
                        last.then_inc(t_full[bank], 1)

                def values(s):
                    banks = (2, 0)
                    for r in range(2):
                        use = ("p", s, r)
                        pe.wait_ge(t_free[bank_of(use)], copied(b, use))
                        if r == 1:
                            pe.wait_ge(ya_ready, START + tile0 + s)
                        for q in range(GRP):
                            h = GRP * r + q
                            mm(ps_w[:, banks[r], q * VW:(q + 1) * VW], probs_t[:, h, :], v_main[:, h, :], q == 0, False)
                    use = ("p", s, 2)
                    pe.wait_ge(t_free[bank_of(use)], copied(b, use))
                    for r in range(2):
                        mm(ps_w[:, banks[r], 0:GRP * VW], probs_t[0:GRP * REM, HEADS + r, :],
                           v_rem[:, r, :, :].rearrange("p q v -> p (q v)"), False, True).then_inc(ov_full, 1)

                def turn_o(s):
                    pe.wait_ge(on_ready, tile0 + s + 1)
                    for bank in range(2):
                        pe.wait_ge(t_free[bank], before(b, ("o", s, bank)))
                    for j in range(KT):
                        last = turned(ps_t_flat[:, j * P:(j + 1) * P], o_norm[:, j * P:(j + 1) * P])
                        if j in (3, 4):
                            last.then_inc(t_full[j - 3], 1)

                def project(s, half):
                    c, t = divmod(s, ST)
                    if half == 0:
                        pe.wait_ge(ot_low, tile0 + s + 1)
                        if t == 0:
                            pe.wait_ge(t_free[bank_of(("gather", c))], copied(b, ("gather", c)))
                    else:
                        pe.wait_ge(y_ready, START + tile0 + s)
                    cols = slice(half * HALF, (half + 1) * HALF)
                    for kt in range(KT):
                        rows = slice(kt * P, (kt + 1) * P)
                        mm3(ps_w[:, half, 0:HALF], ot_h[:, rows], ot_l[:, rows], wo_h[:, kt, cols],
                            wo_l[:, kt, cols], kt == 0, False)
                    mm(ps_w[:, half, 0:HALF], p2_rows[:, t * P:(t + 1) * P], vw2_b[:, cols], False, True).then_inc(y_full, 1)

                turn_for_q(0, range(KT))
                queries(0)
                gather(0)
                tile_scores(0)
                pe.wait_ge(vw2_in, 16 * (b + 1))
                for s in range(SLOTS):
                    c, t = divmod(s, ST)
                    if s + 1 < SLOTS:
                        if t == ST - 1:
                            queries(c + 1)
                        tile_scores(s + 1)
                    turn_weights(s)
                    if s:
                        project(s - 1, 0)
                    if c + 1 < CHUNKS:
                        turn_for_q(c + 1, X_TURNS[t])
                    values(s)
                    if s:
                        project(s - 1, 1)
                    if t == 0 and c:
                        gather(c)
                    turn_o(s)
                project(SLOTS - 1, 0)
                project(SLOTS - 1, 1)

        @block.scalar
        def _(act):
            copy, exp = ACT.Copy, ACT.Exp
            act.wait_ge(su_dve, 6)
            act.wait_ge(vw2_out, 16)
            with act.Fori(0, B) as b:
                act.wait_ge(enc_full, b + 1)
                nc.scalar.activation(enc_t[:, :, :].rearrange("p c k -> p (c k)"), ps_t[:, 0, 0:CT * KEYS], copy).then_inc(enc_ready, 1)
                act.wait_ge(kv_full, b + 1)
                for half in range(2):
                    nc.scalar.activation(v_main[:, half * GRP:(half + 1) * GRP, 0:DH],
                                         ps_w[:, half, 0:HALF].rearrange("p (h d) -> p h d", h=GRP), copy)
                    tail = (ps_s[0:REM, 2, 0:HALF], ps_t[0:REM, 1, 0:HALF])[half]
                    last = nc.scalar.activation(v_tail[:, half * HALF:(half + 1) * HALF], tail, copy)
                last.then_inc(vals_ready, 1)
                with act.Fori(0, CHUNKS // 2) as ip:
                    for k in range(2):
                        n = b * CHUNKS + ip * 2 + k
                        for use in G_ORDER:
                            _, kt, bank = use
                            act.wait_ge(gt_full[bank], g_turn(n, use) + 1)
                            if kt < KT - 1:
                                act.wait_ge(gx_used, n * (KT - 1) + kt + 1)
                            else:
                                act.wait_ge(g_full, START + n)
                            nc.scalar.activation(xt_h[:, kt, :], ps_t[:, bank, :], copy).then_inc(gx_high, 1)

                def head(h, k):
                    hh = b * HEADS + h
                    for st in range(NST):
                        act.wait_ge(sc_full, START + hh * NST + st + 1)
                        act.wait_ge(w_used, hh * NST + st + 1)
                        nc.scalar.activation(caw[:, st % 4, :], ps_w[:, st % 2, 0:CAD], exp, scale=SCALE).then_inc(w_ready, 1)
                    act.wait_ge(w_used, (hh + 1) * NST + 4)
                    nc.scalar.activation(hsu[0:VW, k, :], ps_s[0:VW, 2, 0:CAD], copy).then_inc(hsu_ready, 1)

                with act.Fori(0, HEADS // 2) as hp:
                    head(hp * 2, 0)
                    head(hp * 2 + 1, 1)
                act.wait_ge(s2_ready, START + b + 1)
                nc.scalar.activation(p2[:, :, :], s2[:, :, :], exp, scale=SCALE).then_inc(e2_ready, 1)

                tile0 = b * SLOTS

                def high(dst, use):
                    act.wait_ge(t_full[bank_of(use)], filled(b, use))
                    nc.scalar.activation(dst, ps_t[:, bank_of(use), :], copy).then_inc(t_high, 1)

                def turned_weights(dst, src, use):
                    act.wait_ge(t_full[bank_of(use)], filled(b, use))
                    nc.scalar.activation(dst, src, copy).then_inc(t_free[bank_of(use)], 1)

                def weights(s):
                    act.wait_ge(nmax_ready, tile0 + s + 1)
                    for h in range(HEADS):
                        bank, c = h // 3, h % 3
                        last = nc.scalar.activation(probs[:, h, :], ps_s[:, bank, c * KEYS:(c + 1) * KEYS], exp,
                                                    bias=neg_max[:, s % 2, h:h + 1], scale=SCALE)
                    last.then_inc(p_ready, 1)

                def store(s):
                    act.wait_ge(y_ready, START + tile0 + s + 1)
                    act.dma_start(out_rows[bass.ds(tile0 + s, 1)].rearrange("a p n -> p (a n)"),
                                  o_tile[:, s % 2, :]).then_inc(stored[s % 2], 16)

                for kt in range(KT):
                    high(xt_h[:, kt, :], ("x", 0, kt))
                for j in range(KT):
                    high(qt_h[:, j, :], ("q", 0, j))
                weights(0)
                for s in range(SLOTS):
                    c, t = divmod(s, ST)
                    if t == ST - 1 and c + 1 < CHUNKS:
                        for j in range(KT):
                            high(qt_h[:, j, :], ("q", c + 1, j))
                    use = ("p", s, 0)
                    turned_weights(probs_t[:, 0:GRP, :], ps_t[:, bank_of(use), :].rearrange("p (r s) -> p r s", r=GRP), use)
                    use = ("p", s, 2)
                    turned_weights(probs_t[0:GRP * REM, HEADS:HEADS + 2, :],
                                   ps_t[0:GRP * REM, bank_of(use), 0:2 * P].rearrange("p (r s) -> p r s", r=2), use)
                    if s + 1 < SLOTS:
                        weights(s + 1)
                    if s > 1:
                        store(s - 2)
                    if c + 1 < CHUNKS:
                        for kt in X_TURNS[t]:
                            high(xt_h[:, kt, :], ("x", c + 1, kt))
                    for bank in range(2):
                        act.wait_ge(t_full[bank], filled(b, ("o", s, bank)))
                    nc.scalar.activation(ot_h[:, :], ps_t_flat[:, 0:HID], copy).then_inc(ot_high, 1)
                store(SLOTS - 2)
                store(SLOTS - 1)
            for k in range(2):
                act.wait_ge(stored[k], START + 16 * B * SLOTS // 2)

        @block.vector
        def _(dve):
            v = nc.vector
            dve.wait_ge(su_in, 16 * SETUP_LOADS)
            steps = Steps(dve, dve_setup, 0, 0)
            for started in (s2_ready, y_ready, ya_ready, z_free, hsu_ready, g_ready, g_full, sc_full, *gt_free, *t_free, *stored):
                dve.sem_inc(started, START)
            dve.sem_inc(gx_used, KT - 1)
            dve.sem_inc(w_used, 4)
            v.memset(p2_rows[3 * HT:3 * HT + 2, :].bitcast(F32), 1.0)
            v.memset(v_main[:, :, DH:VW], 1.0)
            v.memset(m2[:, :, :, :], 0.0)
            steps.done(v.memset(v_rem[:, :, :, :], 0.0))
            v.tensor_copy(m2[:, :, :, HT:HT + 1], last_row[:, :].unsqueeze(1).unsqueeze(1).broadcast_to([VW, HEADS, B, 1]))
            for r in range(2):
                v.tensor_copy(v_rem[:, r, :, DH], rem_of[:, :])
            steps.done(v.tensor_copy(wq_h[:, :, :], stage_w))
            v.tensor_tensor(wq_l[:, :, :], stage_w, wq_h[:, :, :], ALU.subtract)
            dve.wait_ge(su_pe, 1)
            for j, src in enumerate((ps_t_flat, ps_s_flat, ps_w_flat)):
                v.tensor_copy(wq_t[j], src[:, 0:HID])
            n = CT * B * TOK + KT * TOK
            steps.done(v.tensor_copy(small_t[:, :], ps_s[:, 2, 0:n]))
            wg_src = wqca_t.unsqueeze(2).broadcast_to([P, KT, HEADS, TOK])
            wg_mask = head_of[:, :, :].unsqueeze(3).broadcast_to([P, KT, HEADS, TOK])
            steps.done(v.tensor_tensor(wg_full.rearrange("p k (h t) -> p k h t", h=HEADS), wg_src, wg_mask, ALU.mult))
            for r in range(3):
                last = v.tensor_copy(wg_h[:, :, r * HT:(r + 1) * HT], wg_full)
            steps.done(last)
            for r in range(3):
                last = v.tensor_tensor(wg_l[:, :, r * HT:(r + 1) * HT], wg_full, wg_h[:, :, 0:HT], ALU.subtract)
            last.then_inc(su_dve, 1)
            dve.wait_ge(su_pe, 2)
            v.tensor_copy(wq_t[3], ps_t_flat[:, 0:HID])
            v.tensor_copy(wq_t[4], ps_s_flat[:, 0:HID])
            steps.done(v.tensor_copy(kv2_t[:, :, :, :].rearrange("p a j n -> p (a j n)"), ps_w[:, 0, 0:2 * KT * B * TOK]))
            for j in range(KT):
                mask = head_of[:, j, :].unsqueeze(1).unsqueeze(3).broadcast_to([P, B, HEADS, TOK])
                k2, v2 = (kv2_t[:, a, j, :].rearrange("p (b t) -> p b t", b=B).unsqueeze(2).broadcast_to([P, B, HEADS, TOK])
                          for a in range(2))
                v.tensor_tensor(k2_bd[:, j, :].rearrange("p (b h t) -> p b h t", b=B, h=HEADS), k2, mask, ALU.mult)
                for r in range(3):
                    last = v.tensor_tensor(v2_bd[:, j, :, r * HT:(r + 1) * HT].rearrange("p b (h t) -> p b h t", h=HEADS),
                                           v2, mask, ALU.mult)
            last.then_inc(su_dve, 1)
            dve.wait_ge(su_pe, 3)
            for a in range(2):
                last = v.tensor_copy(m2[0:DH, a * 4:(a + 1) * 4, :, 0:HT],
                                     ps_s[0:DH, a, :].rearrange("p (h b n) -> p h b n", h=4, b=B))
            last.then_inc(su_dve, 1)
            dve.wait_ge(su_wout_in, 16)
            steps.done(v.tensor_copy(wo_h[:, :, :], stage_w))
            v.tensor_tensor(wo_l[:, :, :], stage_w, wo_h[:, :, :], ALU.subtract)
            for pair in range(B // 2):
                dve.wait_ge(su_pe, 4 + pair)
                for a, src in enumerate((ps_t, ps_w)):
                    dst = vw2[0:3 * HT, 2 * pair + a, :].rearrange("p (a n) -> p a n", a=2)
                    steps.done(v.tensor_copy(dst, src[0:3 * HT, 0:2, 0:HALF]))
                    low = slice(HT, 2 * HT)
                    last = v.tensor_tensor(vw2[low, 2 * pair + a, :].rearrange("p (a n) -> p a n", a=2),
                                           src[low, 0:2, 0:HALF], vw2[low, 2 * pair + a, :].rearrange("p (a n) -> p a n", a=2),
                                           ALU.subtract)
                last.then_inc(su_dve, 1)
            rows = slice(3 * HT, 3 * HT + 2)
            steps.done(v.tensor_copy(vw2[rows, 0, :], bias_in))
            steps.done(v.tensor_tensor(bias_tmp, bias_in, vw2[rows, 0, :], ALU.subtract))
            steps.done(v.tensor_scalar(bias_tmp, bias_tmp, hi_lo[rows, 1:2], None, ALU.mult))
            steps.done(v.scalar_tensor_tensor(bias_in, vw2[rows, 0, :], hi_lo[rows, 0:1], bias_tmp, ALU.mult, ALU.add))
            for b in range(B):
                last = v.tensor_copy(vw2[rows, b, :], bias_in)
            last.then_inc(su_dve, 1)

            def low_x(b, n, k, order, turn, high, free):
                for use in order[0:KT]:
                    _, kt, bank = use
                    dve.wait_ge(high, n * KT + kt + 1)
                    v.tensor_tensor(xt_l[:, kt, :], ps_t[:, bank, :], xt_h[:, kt, :], ALU.subtract).then_inc(free[bank], 1)

            with dve.Fori(0, B) as b:
                dve.wait_ge(kv_full, b + 1)
                steps = Steps(dve, dve_batch, b, 1)
                v.memset(g[3 * HT:3 * HT + 1, :].bitcast(F32), 1.0)
                v.memset(xh[:, :, :, DH:VW], 1.0).then_inc(ones_set, 1)
                for at, (j, h) in enumerate(PAIRS):
                    v.tensor_scalar(keys_h[:, at, :], ps_s[:, j // 3, j % 3 * KEYS:(j % 3 + 1) * KEYS],
                                    head_of[:, j, h:h + 1], None, ALU.mult)
                steps.done(v.tensor_copy(ca_all[:, :], ps_w[0:3 * HT, 2, 0:CAD]))
                steps.close()
                for at, (j, h) in enumerate(PAIRS):
                    v.scalar_tensor_tensor(keys_l[:, at, :], ps_s[:, j // 3, j % 3 * KEYS:(j % 3 + 1) * KEYS],
                                           head_of[:, j, h:h + 1], keys_h[:, at, :], ALU.mult, ALU.subtract)
                low = slice(HT, 2 * HT)
                v.tensor_tensor(ca_all[low, :], ps_w[low, 2, 0:CAD], ca_all[low, :], ALU.subtract).then_inc(keys_ready, 1)

                with dve.Fori(0, CHUNKS // 2) as ip:
                    for k in range(2):
                        i = ip * 2 + k
                        n = b * CHUNKS + i
                        low_x(b, n, k, G_ORDER, g_turn, gx_high, gt_free)
                        dve.wait_ge(g_full, START + n + 1)
                        at = bass.ds(i * CHUNK, CHUNK)
                        v.tensor_copy(g[0:3 * HT, at], ps_w[0:3 * HT, 0, :]).then_inc(g_high, 1)
                        dve.wait_ge(g_high, n + 1)
                        low = slice(2 * HT, 3 * HT)
                        v.tensor_tensor(g[low, at], ps_w[low, 0, :], g[low, at], ALU.subtract).then_inc(g_ready, 1)

                def set_head(h, k):
                    v.tensor_scalar(ca_head[0:3 * HT, k, :], ca_all[:, :],
                                    block_of[:, bass.ds(h, 1)] if not isinstance(h, int) else block_of[:, h:h + 1],
                                    None, ALU.mult).then_inc(head_set, 1)

                def maxima(h, k):
                    first = (b * HEADS + h) * 2 * CT
                    for u in range(2 * CT):
                        dve.wait_ge(max_full, first + u + 1)
                        src = ps_t if u % 2 else ps_s
                        v.tensor_reduce(unit_max[:, k, u:u + 1], src[:, 0:2, :], mybir.AxisListType.XY, ALU.max).then_inc(max_free, 1)
                    dve.wait_ge(max_free, first + 2 * CT)
                    v.tensor_reduce(row_max[:, k, :], unit_max[:, k, :].rearrange("p (c a) -> p c a", a=2), AX_X, ALU.max).then_inc(rmax_ready, 1)
                    dve.wait_ge(rmax_t, b * HEADS + h + 1)
                    v.tensor_scalar(ca_head[3 * HT:3 * HT + 1, k, :], ps_w[0:1, 2, 0:CAD], -1.0, None, ALU.mult).then_inc(head_ready, 1)

                def add_head(h):
                    hh = b * HEADS + h
                    dve.wait_ge(z_full, hh + 1)
                    z = ps_w[0:WIN, 2, 0:CHUNKS * (HT + 1)].rearrange("p (w n) -> p w n", w=CHUNKS)
                    v.reciprocal(z_rec[:, :], z[:, :, HT]).then_inc(z_rec_ready, 1)
                    dve.wait_ge(z_rec_ready, hh + 1)
                    first = isinstance(h, int) and h == 0
                    v.tensor_tensor((s2 if first else z_norm)[:, :, :], z[:, :, 0:HT],
                                    z_rec[:, :].unsqueeze(2).broadcast_to([WIN, CHUNKS, HT]), ALU.mult).then_inc(z_free, 1)
                    dve.wait_ge(z_free, START + hh + 1)
                    if not first:
                        dve.wait_ge(s2_added, b * (HEADS - 1) + h - 1)
                        v.tensor_tensor(s2[:, :, :], s2[:, :, :], z_norm[:, :, :], ALU.add).then_inc(s2_added, 1)

                def head(h, k, first):
                    dve.wait_ge(sc_full, START + (b * HEADS + h) * NST)
                    set_head(h + 1, 1 - k)
                    if not first:
                        add_head(h - 1)
                    maxima(h + 1, 1 - k)

                set_head(0, 0)
                maxima(0, 0)
                head(0, 0, True)
                head(1, 1, False)
                with dve.Fori(1, HEADS // 2 - 1) as hp:
                    head(hp * 2, 0, False)
                    head(hp * 2 + 1, 1, False)
                head(HEADS - 2, 0, False)
                add_head(HEADS - 2)
                add_head(HEADS - 1)
                dve.wait_ge(s2_added, (b + 1) * (HEADS - 1))
                steps = Steps(dve, dve_p2, b, 4)
                by_head = lambda a: a[:, :, :].rearrange("p w (h t) -> p (w h) t", t=TOK)
                spread_t = s2_max[:, :].unsqueeze(2).broadcast_to([WIN, CHUNKS * HEADS, TOK])
                steps.done(v.tensor_reduce(s2_max[:, :], by_head(s2), AX_X, ALU.max))
                v.tensor_tensor(by_head(s2), by_head(s2), spread_t, ALU.subtract).then_inc(s2_ready, 1)
                dve.wait_ge(e2_ready, b + 1)
                steps.done(v.tensor_reduce(s2_max[:, :], by_head(p2), AX_X, ALU.add))
                steps.done(v.reciprocal(s2_max[:, :], s2_max[:, :]))
                steps.done(v.tensor_tensor(by_head(p2), by_head(p2), spread_t, ALU.mult))
                for r in range(3):
                    last = v.tensor_copy(p2_rep[:, :, r, :], p2[:, :, :])
                last.then_inc(p2_ready, 1)
                steps.close()

                tile0 = b * SLOTS
                steps = Steps(dve, dve_tile, b, CHUNKS + 3 * SLOTS)
                dve.wait_ge(p2_ready, b + 1)

                def low(dst, high_part, use):
                    dve.wait_ge(t_high, b * T_HIGHS + T_HIGH[use] + 1)
                    v.tensor_tensor(dst, ps_t[:, bank_of(use), :], high_part, ALU.subtract).then_inc(t_free[bank_of(use)], 1)

                def pick_window(c):
                    v.tensor_copy(p2_chunk[:, :], p2_rep[:, c, :, :].rearrange("p r n -> p (r n)")).then_inc(p2c_ready, 1)

                def picked(c):
                    use = ("gather", c)
                    dve.wait_ge(t_full[bank_of(use)], filled(b, use))
                    steps.done(v.tensor_copy(p2_rows[0:3 * HT, :], ps_t[0:3 * HT, bank_of(use), :]))
                    low_rows = slice(2 * HT, 3 * HT)
                    v.tensor_tensor(p2_rows[low_rows, :], ps_t[low_rows, bank_of(use), :], p2_rows[low_rows, :],
                                    ALU.subtract).then_inc(t_free[bank_of(use)], 1)

                def maximum(s):
                    dve.wait_ge(s_full, tile0 + s + 1)
                    v.tensor_reduce(neg_max[:, s % 2, 0:6].rearrange("p (a h) -> p a h", a=2),
                                    ps_s[:, 0:2, 0:3 * KEYS].rearrange("p a (h k) -> p a h k", h=3), AX_X, ALU.max)
                    steps.done(v.tensor_reduce(neg_max[:, s % 2, 6:8], ps_s[:, 2, 0:2 * KEYS].rearrange("p (h k) -> p h k", h=2),
                                               AX_X, ALU.max))
                    v.tensor_scalar(neg_max[:, s % 2, :], neg_max[:, s % 2, :], -SCALE, None, ALU.mult).then_inc(nmax_ready, 1)

                def remaining(s):
                    dve.wait_ge(p_ready, tile0 + s + 1)
                    v.tensor_copy(probs_rem[:, :, :], probs[:, :, P:KEYS]).then_inc(rem_ready, 1)

                def turned_weights(s):
                    use = ("p", s, 1)
                    dve.wait_ge(t_full[bank_of(use)], filled(b, use))
                    v.tensor_copy(probs_t[:, GRP:HEADS, :],
                                  ps_t[:, bank_of(use), :].rearrange("p (r s) -> p r s", r=GRP)).then_inc(t_free[bank_of(use)], 1)

                def normalise(s):
                    for r in range(2):
                        dve.wait_ge(ov_full, (tile0 + s) * 2 + r + 1)
                        o = ps_w[:, 2 if r == 0 else 0, 0:GRP * VW].rearrange("p (q v) -> p q v", q=GRP)
                        steps.done(v.reciprocal(o_rec[:, r * GRP:(r + 1) * GRP], o[:, :, DH]))
                        last = v.tensor_tensor(o_norm[:, r * HALF:(r + 1) * HALF].rearrange("p (q d) -> p q d", q=GRP),
                                               o[:, :, 0:DH],
                                               o_rec[:, r * GRP:(r + 1) * GRP].unsqueeze(2).broadcast_to([P, GRP, DH]), ALU.mult)
                    last.then_inc(on_ready, 1)

                def add_rows(s, half):
                    c, t = divmod(s, ST)
                    if half == 0:
                        dve.wait_ge(stored[s % 2], START + 16 * (b * (SLOTS // 2) + s // 2))
                    dve.wait_ge(y_full, (tile0 + s) * 2 + half + 1)
                    cols = slice(half * HALF, (half + 1) * HALF)
                    v.tensor_tensor(o_tile[:, s % 2, cols], ps_w[:, half, 0:HALF], xc[:, c % 2 * ST + t, cols],
                                    ALU.add).then_inc((ya_ready, y_ready)[half], 1)

                pick_window(0)
                for kt in range(KT):
                    low(xt_l[:, kt, :], xt_h[:, kt, :], ("x", 0, kt))
                for j in range(KT):
                    low(qt_l[:, j, :], qt_h[:, j, :], ("q", 0, j))
                picked(0)
                maximum(0)
                for s in range(SLOTS):
                    c, t = divmod(s, ST)
                    remaining(s)
                    if t == ST - 1 and c + 1 < CHUNKS:
                        for j in range(KT):
                            low(qt_l[:, j, :], qt_h[:, j, :], ("q", c + 1, j))
                    if s + 1 < SLOTS:
                        maximum(s + 1)
                    turned_weights(s)
                    if s:
                        add_rows(s - 1, 0)
                    if c + 1 < CHUNKS:
                        for kt in X_TURNS[t]:
                            low(xt_l[:, kt, :], xt_h[:, kt, :], ("x", c + 1, kt))
                    if t == 0 and c:
                        pick_window(c)
                    normalise(s)
                    if s:
                        add_rows(s - 1, 1)
                    if t == 0 and c:
                        picked(c)
                    dve.wait_ge(ot_high, tile0 + s + 1)
                    v.tensor_tensor(ot_l[:, :], ps_t_flat[:, 0:HID], ot_h[:, :], ALU.subtract).then_inc(ot_low, 1)
                add_rows(SLOTS - 1, 0)
                add_rows(SLOTS - 1, 1)
                steps.close()


_INS = ["x", "ctx_768", "L0_xattn_Wq", "L0_xattn_Wk", "L0_xattn_Wv", "L0_xattn_Wq_ca", "L0_xattn_Wk_ca",
        "L0_xattn_Wv_ca", "L0_xattn_Wout", "L0_xattn_b_out"]
_CONSTS = ["ident", "head_of", "block_of", "pick", "rem_of", "last_row", "hi_lo", "spread"]


def kernel(**inputs):
    import concourse.bacc as _bacc
    from concourse.bass_utils import run_bass_kernel_spmd as _run

    nc = _bacc.Bacc("TRN2", target_bir_lowering=False, num_devices=1)
    consts = constants()
    arrays, args = {}, []
    for name, a in [(n, inputs[n]) for n in _INS] + [(n, consts[n]) for n in _CONSTS]:
        a = np.ascontiguousarray(a)
        arrays[f"in_{name}_dram"] = a
        args.append(nc.dram_tensor(f"in_{name}_dram", a.shape, mybir.dt.from_np(a.dtype), kind="ExternalInput").ap())
    out = nc.dram_tensor("out_dram", (B, S, HID), F32, kind="ExternalOutput").ap()
    cross_attention(nc, *args, out)
    r = _run(nc, [arrays], core_ids=[0])
    return r.results[0]["out_dram"]
```

```python
from contextlib import ExitStack

import numpy as np

import concourse.bass as bass
from concourse import mybir

F32 = mybir.dt.float32
F32R = mybir.dt.float32r
ACT = mybir.ActivationFunctionType
ALU = mybir.AluOpType
AX_X = mybir.AxisListType.X

B, S, HID = 4, 2048, 640
HEADS, DH = 8, 80
CAD, TOK, CTX = 384, 4, 154
KEYS = CTX - TOK
SCALE = float(DH) ** -0.5

P = 128
KT = HID // P
CT = CAD // P
CHUNK = 512
CHUNKS = S // CHUNK
ST = CHUNK // P
NST = S // P
VW = DH + 1
REM = KEYS - P
GRP = 4
HT = HEADS * TOK
HALF = HID // 2
BH = B * HT

ROW_OF = np.linspace(0, CAD - 1, S).astype(np.int64)
WIN0 = [int(ROW_OF[CHUNK * i]) for i in range(CHUNKS)]
WIN = max(int(ROW_OF[CHUNK * i + CHUNK - 1]) - WIN0[i] + 1 for i in range(CHUNKS))

TILE_HEADS = [[h for h in range(HEADS) if h * DH < (j + 1) * P and (h + 1) * DH > j * P] for j in range(KT)]
PAIRS = [(j, h) for j in range(KT) for h in TILE_HEADS[j]]
PAIR_AT = {jh: n for n, jh in enumerate(PAIRS)}
BANK_HEADS = [[0, 1, 2], [3, 4, 5], [6, 7]]


def score_runs():
    runs = []
    for bank, heads in enumerate(BANK_HEADS):
        for j in range(KT):
            own = [h for h in TILE_HEADS[j] if h in heads]
            if own:
                runs.append((bank, j, own[0], len(own)))
    return runs


RUNS = score_runs()

SLOTS = S // P


def turns():
    order = [("x", 0, kt) for kt in range(KT)] + [("q", 0, j) for j in range(KT)] + [("gather", 0)]
    for s in range(SLOTS):
        c, t = divmod(s, ST)
        ahead = c + 1 < CHUNKS
        if t == ST - 1 and ahead:
            order += [("q", c + 1, j) for j in range(KT)]
        order += [("p", s, part) for part in range(3)]
        if ahead:
            order += [("x", c + 1, kt) for kt in X_EARLY[t] + X_LATE[t]]
            if t == GATHER_AT:
                order.append(("gather", c + 1))
        order += [("o", s, 0), ("o", s, 1)]
    used, copied, use, bank = [0, 0], [0, 0], {}, 1
    for name in order:
        bank = name[2] if name[0] == "o" else 1 - bank
        use[name] = (bank, used[bank], copied[bank])
        used[bank] += 1
        copied[bank] += name[0] != "o"
    return use, used, copied


X_EARLY = [[], [0], [2], []]
X_LATE = [[], [1], [3, 4], []]
GATHER_AT = 1
T_USE, T_USED, T_COPIED = turns()
T_HIGH = {}
for _use in T_USE:
    if _use[0] in "xq":
        T_HIGH[_use] = len(T_HIGH)
T_HIGHS = len(T_HIGH)
START = 1
GX = CHUNKS * KT
GX_BANKS = 4
GX_LAG = 3


def constants():
    ident = np.eye(P, dtype=np.float32)
    head_of = np.zeros((P, KT, HEADS), np.float32)
    for j in range(KT):
        for p in range(P):
            head_of[p, j, (j * P + p) // DH] = 1
    block_of = np.zeros((3 * HT, HEADS), np.float32)
    for p in range(3 * HT):
        block_of[p, (p % HT) // TOK] = 1
    pick = np.zeros((CHUNKS, WIN, CHUNK), np.float32)
    for s in range(S):
        pick[s // CHUNK, ROW_OF[s] - WIN0[s // CHUNK], s % CHUNK] = 1
    rem_of = np.zeros((GRP * REM, GRP), np.float32)
    for p in range(GRP * REM):
        rem_of[p, p // REM] = 1
    last_row = np.zeros((VW, 1), np.float32)
    last_row[DH] = 1
    hi_lo = np.eye(2, dtype=np.float32)
    spread = np.tile(np.eye(TOK, dtype=np.float32), (1, 3 * HEADS))
    return {"spread": spread, "ident": ident, "head_of": head_of, "block_of": block_of, "pick": pick, "rem_of": rem_of,
            "last_row": last_row, "hi_lo": hi_lo}


class Steps:

    def __init__(self, eng, sem, rounds, per_round):
        self.eng, self.sem, self.base, self.per_round, self.n = eng, sem, rounds * per_round, per_round, 0

    def done(self, instruction):
        instruction.then_inc(self.sem, 1)
        self.n += 1
        self.eng.wait_ge(self.sem, self.base + self.n)

    def close(self):
        assert self.n == self.per_round, (self.n, self.per_round)


def cross_attention(nc, x, ctx, Wq, Wk, Wv, Wq_ca, Wk_ca, Wv_ca, Wout, b_out,
                    c_ident, c_head_of, c_block_of, c_pick, c_rem_of, c_last_row, c_hi_lo, c_spread, out):
    with ExitStack() as stack:
        def sb(name, shape, dt=F32):
            return stack.enter_context(nc.sbuf_tensor(name, shape, dt))

        def sem(name):
            return stack.enter_context(nc.semaphore(name))

        ident = sb("ident", [P, P])
        head_of = sb("head_of", [P, KT, HEADS])
        block_of = sb("block_of", [3 * HT, HEADS])
        rem_of = sb("rem_of", [GRP * REM, GRP])
        last_row = sb("last_row", [VW, 1])
        spread = sb("spread", [TOK, 3 * HT])
        hi_lo = sb("hi_lo", [P, 2])
        wq_h, wq_l = sb("wq_h", [P, KT, HID], F32R), sb("wq_l", [P, KT, HID], F32R)
        wo_h, wo_l = sb("wo_h", [P, KT, HID], F32R), sb("wo_l", [P, KT, HID], F32R)
        wg_h, wg_l = sb("wg_h", [P, KT, 3 * HT], F32R), sb("wg_l", [P, KT, 3 * HT], F32R)
        m2 = sb("m2", [VW, HEADS, B, HT + 1])
        vw2_b = sb("vw2_b", [3 * HT + 2, HID], F32R)
        vw2_all = nc.dram_tensor("vw2_all", (3, B * HT, HID), F32, kind="Internal").ap()
        xc = sb("xc", [P, 2 * ST, HID])
        xt_h, xt_l = sb("xt_h", [P, KT, CHUNK], F32R), sb("xt_l", [P, KT, CHUNK], F32R)
        cawork = sb("cawork", [P, 2 * NST * VW + 4 * CAD])
        xh = cawork[:, 0:2 * NST * VW].rearrange("p (k s v) -> p k s v", k=2, s=NST)
        caw = cawork[:, 2 * NST * VW:].rearrange("p (k c) -> p k c", k=4)
        wk = cawork[:, 0:CT * HID].rearrange("p (k n) -> p k n", k=CT)
        wv = cawork[:, CT * HID:2 * CT * HID].rearrange("p (k n) -> p k n", k=CT)
        ca_rows4 = sb("ca_rows4", [TOK, CAD])
        ca_all = sb("ca_all", [3 * HT, CAD], F32R)
        ca_head = sb("ca_head", [3 * HT + 1, 2, CAD], F32R)
        hsu = sb("hsu", [P, 2, CAD])
        ctx_in = hsu
        enc_t = sb("enc_t", [P, CT, KEYS])
        unit_max = sb("unit_max", [P, 2, 2 * CT])
        row_max = sb("row_max", [P, 2, CT])
        z_rec = sb("z_rec", [WIN, CHUNKS])
        z_norm = sb("z_norm", [WIN, CHUNKS, HT])
        s2 = sb("s2", [WIN, CHUNKS, HT])
        s2_max = sb("s2_max", [WIN, CHUNKS * HEADS])
        p2 = sb("p2", [WIN, CHUNKS, HT])
        p2_rep = sb("p2_rep", [WIN, CHUNKS, 3, HT])
        p2_chunk = sb("p2_chunk", [WIN, 3 * HT])
        pick = sb("pick", [WIN, CHUNK])
        p2_rows = sb("p2_rows", [3 * HT + 2, 2, CHUNK], F32R)
        keys_h, keys_l = sb("keys_h", [P, len(PAIRS), KEYS], F32R), sb("keys_l", [P, len(PAIRS), KEYS], F32R)
        v_main = sb("v_main", [P, HEADS, VW])
        v_rem = sb("v_rem", [GRP * REM, 2, GRP, VW])
        v_tail = sb("v_tail", [REM, HID])
        qt_h, qt_l = sb("qt_h", [P, KT, CHUNK], F32R), sb("qt_l", [P, KT, CHUNK], F32R)
        g = qt_l[0:3 * HT + 1, 0:CHUNKS, :].rearrange("p j s -> p (j s)")
        o_norm = sb("o_norm", [P, HID])
        probs = sb("probs", [P, HEADS, KEYS])
        probs_rem = sb("probs_rem", [P, HEADS, REM])
        probs_t = sb("probs_t", [P, HEADS + 2, P])
        neg_max = sb("neg_max", [P, 2, HEADS])
        o_rec = sb("o_rec", [P, HEADS])
        ot_h, ot_l = sb("ot_h", [P, 2, HID], F32R), sb("ot_l", [P, 2, HID], F32R)
        o_tile = sb("o_tile", [P, 2, HID])
        stage_w = xc[:, 0:KT, :]
        wq_t = [xc[:, KT + j, :] for j in range(3)] + [o_norm[:, :], probs_t[:, 5:10, :].rearrange("p a b -> p (a b)")]
        vw2_h, vw2_l = ot_h[:, 0, :], ot_l[:, 0, :]
        m2_rows = o_tile[:, 1, :]
        k2_bd = probs_t[:, 0:KT, :]
        wqca_in, bias_in, ca_rows = o_tile[0:TOK, 0, :], o_tile[3 * HT:3 * HT + 2, 0, :], o_tile[0:B * TOK, 1, 0:CAD]
        bias_tmp = o_tile[3 * HT:3 * HT + 2, 1, :]
        probs_flat = probs[:, :, :].rearrange("p a b -> p (a b)")
        small_n, kv2_n = CT * B * TOK + KT * TOK, 2 * KT * B * TOK
        small_t = probs_flat[:, 0:small_n]
        ca_t = small_t[:, 0:CT * B * TOK].rearrange("p (k n) -> p k n", k=CT)
        wqca_t = small_t[:, CT * B * TOK:].rearrange("p (k n) -> p k n", k=KT)
        kv2_t = probs_flat[:, small_n:small_n + kv2_n].rearrange("p (a j n) -> p a j n", a=2, j=KT)
        wg_full = probs_flat[:, small_n + kv2_n:small_n + kv2_n + KT * HT].rearrange("p (k n) -> p k n", k=KT)

        v2_at = small_n + kv2_n + KT * HT
        v2_bd = probs_flat[:, v2_at:v2_at + KT * BH].rearrange("p (k n) -> p k n", k=KT)

        ps_t = stack.enter_context(nc.psum_tensor("ps_t", [P, 2, 512], F32))
        ps_s = stack.enter_context(nc.psum_tensor("ps_s", [P, 3, 512], F32))
        ps_w = stack.enter_context(nc.psum_tensor("ps_w", [P, 3, 512], F32))
        ps_t_flat = ps_t[:, :, :].rearrange("p a b -> p (a b)")
        ps_s_flat = ps_s[:, :, :].rearrange("p a b -> p (a b)")
        ps_w_flat = ps_w[:, :, :].rearrange("p a b -> p (a b)")

        su_in, su_wq_in, su_wout_in = sem("su_in"), sem("su_wq_in"), sem("su_wout_in")
        su_turned, kv2_full, m2_rows_full, vw2_full, m2_full = (
            sem("su_turned"), sem("kv2_full"), sem("m2_rows_full"), sem("vw2_full"), sem("m2_full"))
        su_turned_ready, kv2_ready, m2_rows_ready, vw2_ready, m2_ready, wo_ready = (
            sem("su_turned_ready"), sem("kv2_ready"), sem("m2_rows_ready"), sem("vw2_ready"), sem("m2_ready"),
            sem("wo_ready"))
        dve_setup, dve_batch, dve_p2, dve_tile = (
            sem("dve_setup"), sem("dve_batch"), sem("dve_p2"), sem("dve_tile"))
        kv_in, enc_full, enc_ready, kv_full, keys_ready, vals_ready, v_rem_in = (
            sem("kv_in"), sem("enc_full"), sem("enc_ready"), sem("kv_full"), sem("keys_ready"),
            sem("vals_ready"), sem("v_rem_in"))
        ones_set = sem("ones_set")
        xc_in = [sem("xc_in0"), sem("xc_in1")]
        gx_turned, gx_high, gx_low, gx_used, g_high, g_ready = (
            sem("gx_turned"), sem("gx_high"), sem("gx_low"), sem("gx_used"), sem("g_high"), sem("g_ready"))
        ca_ready, keys_high = sem("ca_ready"), sem("keys_high")
        xh_in = [sem("xh_in0"), sem("xh_in1")]
        head_set, max_full, max_free, rmax_ready, rmax_t, head_ready = (
            sem("head_set"), sem("max_full"), sem("max_free"), sem("rmax_ready"), sem("rmax_t"), sem("head_ready"))
        sc_full, w_ready, w_used, hsu_ready, z_full, z_free = (
            sem("sc_full"), sem("w_ready"), sem("w_used"), sem("hsu_ready"), sem("z_full"),
            sem("z_free"))
        z_rec_ready, s2_added = sem("z_rec_ready"), sem("s2_added")
        s2_ready, e2_ready, p2_ready = sem("s2_ready"), sem("e2_ready"), sem("p2_ready")
        pick_in, p2c_ready = sem("pick_in"), sem("p2c_ready")
        vw2_out, vw2_in, t_high = sem("vw2_out"), sem("vw2_in"), sem("t_high")
        t_full, t_free = [sem("t_full0"), sem("t_full1")], [sem("t_free0"), sem("t_free1")]
        s_full, nmax_ready, p_ready, rem_ready = sem("s_full"), sem("nmax_ready"), sem("p_ready"), sem("rem_ready")
        ov_full, on_ready, ot_high, ot_low, y_full, ya_ready, y_ready = (
            sem("ov_full"), sem("on_ready"), sem("ot_high"), sem("ot_low"), sem("y_full"),
            sem("ya_ready"), sem("y_ready"))
        stored = [sem("stored0"), sem("stored1")]

        x_rows = x.rearrange("b (c t p) n -> (b c) p t n", t=ST, p=P)
        x_heads = x.rearrange("b (s p) n -> b p s n", p=P)
        out_rows = out.rearrange("b (n p) h -> (b n) p h", p=P)
        SETUP_LOADS = 15
        KV_LOADS = 5

        block = stack.enter_context(nc.Block())

        def bank_of(use):
            return T_USE[use][0]

        def filled(b, use):
            return b * T_USED[T_USE[use][0]] + T_USE[use][1] + 1

        def before(b, use):
            return START + b * T_COPIED[T_USE[use][0]] + T_USE[use][2]

        def copied(b, use):
            return before(b, use) + 1

        gx_banks = [ps_t[:, 0, :], ps_t[:, 1, :], ps_s[:, 2, :], ps_w[:, 1, :]]
        g_banks = [ps_w[0:3 * HT, 0, :], ps_w[0:3 * HT, 2, :]]

        @block.sync
        def _(sp):
            sp.dma_start(ident[:, :], c_ident).then_inc(su_wq_in, 16)
            sp.dma_start(stage_w, Wq.rearrange("(k p) n -> p k n", p=P)).then_inc(su_wq_in, 16)
            sp.dma_start(wk, Wk_ca.rearrange("(k p) n -> p k n", p=P)).then_inc(su_in, 16)
            sp.dma_start(wv, Wv_ca.rearrange("(k p) n -> p k n", p=P)).then_inc(su_in, 16)
            sp.wait_ge(kv2_ready, 1)
            sp.dma_start(stage_w, Wout.rearrange("(k p) n -> p k n", p=P)).then_inc(su_wout_in, 16)

            with sp.Fori(0, B) as b:
                sp.wait_ge(s2_ready, START + b)
                sp.dma_start(wk, Wk.rearrange("(k p) n -> p k n", p=P)).then_inc(kv_in, 16)
                sp.dma_start(wv, Wv.rearrange("(k p) n -> p k n", p=P)).then_inc(kv_in, 16)
                sp.dma_start(ctx_in[:, 0, :], ctx[bass.ds(b, 1), 0:P, :].rearrange("a p n -> p (a n)")).then_inc(kv_in, 16)
                sp.dma_start(ctx_in[0:REM, 1, :],
                             ctx[bass.ds(b, 1), P:KEYS, :].rearrange("a p n -> p (a n)")).then_inc(kv_in, 16)
                sp.dma_start(ca_rows4[:, :],
                             ctx[bass.ds(b, 1), KEYS:CTX, :].rearrange("a p n -> p (a n)")).then_inc(kv_in, 16)

                def load_x(i, k):
                    sp.dma_start(xc[:, k * ST:(k + 1) * ST, :],
                                 x_rows[bass.ds(b * CHUNKS + i, 1)].rearrange("a p t n -> p (a t) n")).then_inc(xc_in[k], 16)

                def load_head(h, k):
                    sp.dma_start(xh[:, k, :, 0:DH],
                                 x_heads[bass.ds(b, 1), :, :, bass.ds(h * DH, DH)].rearrange("a p s d -> p (a s) d")).then_inc(xh_in[k], 16)

                sp.wait_ge(y_ready, START + b * NST)
                sp.wait_ge(wo_ready, 1)
                load_x(0, 0)
                load_x(1, 1)
                for i in range(2, CHUNKS):
                    sp.wait_ge(gx_turned, b * GX + (i - 1) * KT)
                    load_x(i, i % 2)
                sp.wait_ge(vw2_out, 16 * 3)
                for r in range(3):
                    sp.dma_start(vw2_b[r * HT:(r + 1) * HT, :].bitcast(F32), vw2_all[r, bass.ds(b * HT, HT), :]).then_inc(vw2_in, 16)
                sp.wait_ge(vals_ready, b + 1)
                for q in range(GRP):
                    sp.dma_start(v_rem[q * REM:(q + 1) * REM, :, q, 0:DH],
                                 v_tail[:, :].rearrange("p (r q d) -> p r q d", r=2, q=GRP)[:, :, q, :]).then_inc(v_rem_in, 16)
                sp.wait_ge(ones_set, b + 1)
                load_head(0, 0)
                load_head(1, 1)
                for i in range(2):
                    sp.wait_ge(gx_turned, b * GX + (i + 3) * KT)
                    load_x(i, i)
                with sp.Fori(1, HEADS // 2) as hp:
                    for k in range(2):
                        sp.wait_ge(w_used, (b * HEADS + hp * 2 + k - 1) * NST + 4)
                        load_head(hp * 2 + k, k)
                for c in range(CHUNKS):
                    if c:
                        sp.wait_ge(t_full[bank_of(("gather", c - 1))], filled(b, ("gather", c - 1)))
                    sp.dma_start(pick[:, :], c_pick[c]).then_inc(pick_in, 16)
                    if 1 <= c < CHUNKS - 1:
                        sp.wait_ge(y_ready, START + b * SLOTS + c * ST)
                        load_x(c + 1, (c + 1) % 2)

        @block.tensor
        def _(pe):
            def mm(out, lhs, rhs, start, stop):
                return nc.tensor.matmul(out, lhs, rhs, start=start, stop=stop, skip_group_check=True)

            def mm3(out, lhs_h, lhs_l, rhs_h, rhs_l, start, stop):
                mm(out, lhs_h, rhs_h, start, False)
                mm(out, lhs_h, rhs_l, False, False)
                return mm(out, lhs_l, rhs_h, False, stop)

            def turned(out, in_):
                k = in_.shape[0]
                return nc.tensor.transpose(out, in_, ident[0:k, 0:k])

            pe.wait_ge(su_wq_in, 16 * 2)

            def turn_wq(dst, j):
                for k in range(KT):
                    last = turned(dst[:, k * P:(k + 1) * P], stage_w[:, k, j * P:(j + 1) * P])
                return last

            turn_wq(ps_t_flat, 0)
            turn_wq(ps_s_flat, 1)
            turn_wq(ps_w_flat, 2)
            pe.wait_ge(su_in, 16 * SETUP_LOADS)
            for c in range(CT):
                turned(ps_s[:, 2, c * B * TOK:(c + 1) * B * TOK], ca_rows[:, c * P:(c + 1) * P])
            for k in range(KT):
                at = CT * B * TOK + k * TOK
                last = turned(ps_s[:, 2, at:at + TOK], wqca_in[:, k * P:(k + 1) * P])
            last.then_inc(su_turned, 1)
            pe.wait_ge(su_turned_ready, 1)
            turn_wq(ps_t_flat, 3)
            turn_wq(ps_s_flat, 4)
            for n, w in enumerate((wk, wv)):
                for j in range(KT):
                    at = (n * KT + j) * B * TOK
                    for c in range(CT):
                        last = mm(ps_w[:, 0, at:at + B * TOK], w[:, c, j * P:(j + 1) * P], ca_t[:, c, :], c == 0, c == CT - 1)
            last.then_inc(kv2_full, 1)
            pe.wait_ge(kv2_ready, 1)
            for half in range(2):
                for j in range(KT):
                    last = mm(ps_s[:, half, 0:HALF], k2_bd[:, j, :], wq_t[j][:, half * HALF:(half + 1) * HALF], j == 0, j == KT - 1)
            last.then_inc(m2_rows_full, 1)
            pe.wait_ge(su_wout_in, 16)
            for half in range(2):
                for j in range(KT):
                    last = mm(ps_t[:, half, 0:HALF], v2_bd[:, j, :], stage_w[:, j, half * HALF:(half + 1) * HALF], j == 0, j == KT - 1)
            last.then_inc(vw2_full, 1)
            pe.wait_ge(m2_rows_ready, 1)
            for h in range(HEADS):
                last = turned(ps_w[0:DH, h // 4, h % 4 * BH:(h % 4 + 1) * BH], m2_rows[:, h * DH:(h + 1) * DH])
            last.then_inc(m2_full, 1)
            pe.wait_ge(vw2_ready, 1)
            pe.wait_ge(m2_ready, 1)

            def turn_x(k, kt, bank, full):
                for t in range(ST):
                    last = turned(bank[:, t * P:(t + 1) * P], xc[:, k * ST + t, kt * P:(kt + 1) * P])
                last.then_inc(full, 1)

            with pe.Fori(0, B) as b:
                pe.wait_ge(kv_in, 16 * KV_LOADS * (b + 1))
                pe.wait_ge(y_ready, START + b * NST)
                for c in range(CT):
                    turned(ps_t[:, 0, c * KEYS:c * KEYS + P], ctx_in[:, 0, c * P:(c + 1) * P])
                    last = turned(ps_t[:, 0, c * KEYS + P:(c + 1) * KEYS], ctx_in[0:REM, 1, c * P:(c + 1) * P])
                last.then_inc(enc_full, 1)
                pe.wait_ge(enc_ready, b + 1)
                for j in range(KT):
                    for c in range(CT):
                        mm(ps_s[:, j // 3, j % 3 * KEYS:(j % 3 + 1) * KEYS], wk[:, c, j * P:(j + 1) * P],
                           enc_t[:, c, :], c == 0, c == CT - 1)
                for half in range(2):
                    cols = slice(half * HALF, (half + 1) * HALF)
                    tail = (ps_s[0:REM, 2, 0:HALF], ps_t[0:REM, 1, 0:HALF])[half]
                    for c in range(CT):
                        mm(ps_w[:, half, 0:HALF], enc_t[:, c, 0:P], wv[:, c, cols], c == 0, c == CT - 1)
                    for c in range(CT):
                        mm(tail, enc_t[:, c, P:KEYS], wv[:, c, cols], c == 0, c == CT - 1)
                mm(ps_w[0:3 * HT, 2, 0:CAD], spread[:, :], ca_rows4[:, :], True, True).then_inc(kv_full, 1)

                pe.wait_ge(vals_ready, b + 1)
                for m in range(GX + GX_LAG):
                    if m < GX:
                        i, kt = divmod(m, KT)
                        if kt == 0:
                            pe.wait_ge(xc_in[i % 2], 16 * (b * CHUNKS + i // 2 + 1))
                        if m >= GX_BANKS:
                            pe.wait_ge(gx_low, b * GX + m - GX_BANKS + 1)
                        turn_x(i % 2, kt, gx_banks[m % GX_BANKS], gx_turned)
                    if m >= GX_LAG:
                        i, kt = divmod(m - GX_LAG, KT)
                        pe.wait_ge(gx_low, b * GX + m - GX_LAG + 1)
                        if kt == 0 and i == 1:
                            pe.wait_ge(ca_ready, b + 1)
                        if kt == 0 and i > 1:
                            pe.wait_ge(g_ready, b * CHUNKS + i - 1)
                        mm3(g_banks[i % 2], wg_h[:, kt, :], wg_l[:, kt, :], xt_h[:, kt, :], xt_l[:, kt, :], kt == 0,
                            kt == KT - 1).then_inc(gx_used, 1)

                def max_unit(h, k, u):
                    c, half = u // 2, u % 2
                    if not (isinstance(h, int) and h == 0 and u < 2):
                        pe.wait_ge(max_free, (b * HEADS + h) * 2 * CT + u - 1)
                    dst = ps_t if half else ps_s
                    for m in range(2):
                        s0 = (half * 2 + m) * 512
                        last = mm(dst[:, m, :], ca_head[0:3 * HT, k, c * P:(c + 1) * P], g[0:3 * HT, s0:s0 + 512], True, True)
                    last.then_inc(max_full, 1)

                def turn_max(h, k):
                    pe.wait_ge(rmax_ready, b * HEADS + h + 1)
                    pe.wait_ge(z_free, START + b * HEADS + (h - 1 if not isinstance(h, int) or h else 0))
                    for c in range(CT):
                        last = nc.tensor.transpose(ps_w[0:1, 2, c * P:(c + 1) * P], row_max[:, k, c:c + 1], ident[:, :])
                    last.then_inc(rmax_t, 1)

                def weights_sum(h, k):
                    pe.wait_ge(hsu_ready, START + b * HEADS + h + 1)
                    pe.wait_ge(z_free, START + b * HEADS + h)
                    for w in range(CHUNKS):
                        last = mm(ps_w[0:WIN, 2, w * (HT + 1):(w + 1) * (HT + 1)], hsu[0:VW, k, WIN0[w]:WIN0[w] + WIN],
                                  m2[:, h, b, :] if isinstance(h, int) and isinstance(b, int) else
                                  m2[:, bass.ds(h, 1), bass.ds(b, 1), :].rearrange("p a c n -> p (a c n)"), True, True)
                    last.then_inc(z_full, 1)

                def scores(h, k, st):
                    mm(ps_w[:, st % 2, 0:CAD], g[:, st * P:(st + 1) * P], ca_head[:, k, :], True, True).then_inc(sc_full, 1)

                def head(h, k, first, last_one):
                    hh = b * HEADS + h
                    if not last_one:
                        pe.wait_ge(head_set, hh + 2)
                        max_unit(h + 1, 1 - k, 0)
                        max_unit(h + 1, 1 - k, 1)
                    pe.wait_ge(xh_in[k], 16 * (b * (HEADS // 2) + (h // 2 if isinstance(h, int) else hp) + 1))
                    for st in range(NST):
                        pe.wait_ge(w_ready, hh * NST + st + 1)
                        if st == 0:
                            pe.wait_ge(hsu_ready, START + hh)
                        mm(ps_s[0:VW, 2, 0:CAD], xh[:, k, st, :], caw[:, st % 4, :], st == 0, st == NST - 1).then_inc(w_used, 1)
                        if st + 2 < NST:
                            scores(h, k, st + 2)
                        if st == 3 and not first:
                            weights_sum(h - 1, 1 - k)
                        if not last_one:
                            if st % 2 == 0 and 0 < st < 10:
                                max_unit(h + 1, 1 - k, st // 2 + 1)
                            if st == 12:
                                turn_max(h + 1, 1 - k)
                            if st == NST - 2:
                                pe.wait_ge(head_ready, hh + 2)
                            if st >= NST - 2:
                                scores(h + 1, 1 - k, st + 2 - NST)

                pe.wait_ge(keys_ready, b + 1)
                pe.wait_ge(g_ready, (b + 1) * CHUNKS)
                pe.wait_ge(head_set, b * HEADS + 1)
                for u in range(2 * CT):
                    max_unit(0, 0, u)
                turn_max(0, 0)
                pe.wait_ge(head_ready, b * HEADS + 1)
                scores(0, 0, 0)
                scores(0, 0, 1)
                hp = 0
                head(0, 0, True, False)
                head(1, 1, False, False)
                with pe.Fori(1, HEADS // 2 - 1) as hp:
                    head(hp * 2, 0, False, False)
                    head(hp * 2 + 1, 1, False, False)
                head(HEADS - 2, 0, False, False)
                head(HEADS - 1, 1, False, True)
                weights_sum(HEADS - 1, 1)

                pe.wait_ge(z_free, START + (b + 1) * HEADS)
                pe.wait_ge(v_rem_in, 16 * GRP * (b + 1))
                tile0, chunk0 = b * SLOTS, b * CHUNKS

                def turn_for_q(c, kts):
                    if 0 in kts:
                        pe.wait_ge(xc_in[c % 2], 16 * (b * CHUNKS + 2 + c // 2 + 1))
                    for kt in kts:
                        use = ("x", c, kt)
                        pe.wait_ge(t_free[bank_of(use)], before(b, use))
                        turn_x(c % 2, kt, ps_t[:, bank_of(use), :], t_full[bank_of(use)])

                def queries(c):
                    if c:
                        pe.wait_ge(ot_low, tile0 + c * ST - 1)
                    for j in range(KT):
                        use = ("q", c, j)
                        if j == 0:
                            pe.wait_ge(t_free[bank_of(use)], before(b, use))
                            pe.wait_ge(t_free[1 - bank_of(use)], before(b, ("q", c, 1)))
                        elif j > 1:
                            pe.wait_ge(t_free[bank_of(use)], before(b, use))
                        cols = slice(j * P, (j + 1) * P)
                        for kt in range(KT):
                            last = mm3(ps_t[:, bank_of(use), :], wq_h[:, kt, cols], wq_l[:, kt, cols], xt_h[:, kt, :],
                                       xt_l[:, kt, :], kt == 0, kt == KT - 1)
                        last.then_inc(t_full[bank_of(use)], 1)

                def gather(c):
                    use = ("gather", c)
                    pe.wait_ge(pick_in, 16 * (chunk0 + c + 1))
                    pe.wait_ge(p2c_ready, chunk0 + c + 1)
                    pe.wait_ge(t_free[bank_of(use)], before(b, use))
                    mm(ps_t[0:3 * HT, bank_of(use), :], p2_chunk[:, :], pick[:, :], True, True).then_inc(t_full[bank_of(use)], 1)

                def tile_scores(s):
                    c, t = divmod(s, ST)
                    if s:
                        pe.wait_ge(p_ready, tile0 + s)
                    seen = None
                    for bank, j, h0, hs in RUNS:
                        if t == 0:
                            pe.wait_ge(t_free[bank_of(("q", c, j))], copied(b, ("q", c, j)))
                        c0 = (h0 - BANK_HEADS[bank][0]) * KEYS
                        at = PAIR_AT[(j, h0)]
                        rows = slice(t * P, (t + 1) * P)
                        last = mm3(ps_s[:, bank, c0:c0 + hs * KEYS], qt_h[:, j, rows], qt_l[:, j, rows],
                                   keys_h[:, at:at + hs, :].rearrange("p h k -> p (h k)"),
                                   keys_l[:, at:at + hs, :].rearrange("p h k -> p (h k)"), bank != seen, True)
                        seen = bank
                    last.then_inc(s_full, 1)

                def turn_weights(s, parts):
                    if parts[0] == 0:
                        if s:
                            pe.wait_ge(ot_low, tile0 + s)
                        pe.wait_ge(p_ready, tile0 + s + 1)
                    else:
                        pe.wait_ge(rem_ready, tile0 + s + 1)
                    for part in parts:
                        use = ("p", s, part)
                        bank = bank_of(use)
                        pe.wait_ge(t_free[bank], before(b, use))
                        if part < 2:
                            for q in range(GRP):
                                last = turned(ps_t[:, bank, q * P:(q + 1) * P], probs[:, GRP * part + q, 0:P])
                        else:
                            for r in range(2):
                                last = turned(ps_t[0:GRP * REM, bank, r * P:(r + 1) * P],
                                              probs_rem[:, GRP * r:GRP * (r + 1), :].rearrange("p q k -> p (q k)"))
                        last.then_inc(t_full[bank], 1)

                def values(s):
                    banks = (2, 0)
                    for r in range(2):
                        use = ("p", s, r)
                        pe.wait_ge(t_free[bank_of(use)], copied(b, use))
                        if r == 1:
                            pe.wait_ge(ya_ready, START + tile0 + s)
                        for q in range(GRP):
                            h = GRP * r + q
                            mm(ps_w[:, banks[r], q * VW:(q + 1) * VW], probs_t[:, h, :], v_main[:, h, :], q == 0, False)
                    use = ("p", s, 2)
                    pe.wait_ge(t_free[bank_of(use)], copied(b, use))
                    for r in range(2):
                        mm(ps_w[:, banks[r], 0:GRP * VW], probs_t[0:GRP * REM, HEADS + r, :],
                           v_rem[:, r, :, :].rearrange("p q v -> p (q v)"), False, True).then_inc(ov_full, 1)

                def turn_o(s):
                    pe.wait_ge(on_ready, tile0 + s + 1)
                    for bank in range(2):
                        pe.wait_ge(t_free[bank], before(b, ("o", s, bank)))
                    for j in range(KT):
                        last = turned(ps_t_flat[:, j * P:(j + 1) * P], o_norm[:, j * P:(j + 1) * P])
                        if j in (3, 4):
                            last.then_inc(t_full[j - 3], 1)

                def project(s, half, kts=range(KT)):
                    c, t = divmod(s, ST)
                    if kts[0] == 0 and half == 0:
                        pe.wait_ge(ot_low, tile0 + s + 1)
                        if t == 0:
                            pe.wait_ge(t_free[bank_of(("gather", c))], copied(b, ("gather", c)))
                    if kts[0] == 0 and half == 1:
                        pe.wait_ge(y_ready, START + tile0 + s)
                    cols = slice(half * HALF, (half + 1) * HALF)
                    for kt in kts:
                        rows = slice(kt * P, (kt + 1) * P)
                        mm3(ps_w[:, half, 0:HALF], ot_h[:, s % 2, rows], ot_l[:, s % 2, rows], wo_h[:, kt, cols],
                            wo_l[:, kt, cols], kt == 0, False)
                    if kts[-1] == KT - 1:
                        mm(ps_w[:, half, 0:HALF], p2_rows[:, c % 2, t * P:(t + 1) * P], vw2_b[:, cols], False,
                           True).then_inc(y_full, 1)

                turn_for_q(0, range(KT))
                queries(0)
                gather(0)
                tile_scores(0)
                pe.wait_ge(vw2_in, 16 * 3 * (b + 1))
                for s in range(SLOTS):
                    c, t = divmod(s, ST)
                    if s + 1 < SLOTS:
                        if t == ST - 1:
                            queries(c + 1)
                        tile_scores(s + 1)
                    turn_weights(s, (0, 1))
                    if s:
                        project(s - 1, 0)
                    turn_weights(s, (2,))
                    if c + 1 < CHUNKS:
                        turn_for_q(c + 1, X_EARLY[t])
                    values(s)
                    if c + 1 < CHUNKS:
                        turn_for_q(c + 1, X_LATE[t])
                        if t == GATHER_AT:
                            gather(c + 1)
                    if s:
                        project(s - 1, 1, range(0, 2))
                    turn_o(s)
                    if s:
                        project(s - 1, 1, range(2, KT))
                project(SLOTS - 1, 0)
                project(SLOTS - 1, 1)

        @block.scalar
        def _(act):
            copy, exp = ACT.Copy, ACT.Exp
            for dst, src in (
                (o_tile[0:TOK, 0, :], Wq_ca), (head_of[:, :, :], c_head_of), (block_of[:, :], c_block_of),
                (rem_of[:, :], c_rem_of), (last_row[:, :], c_last_row),
                (hi_lo[3 * HT:3 * HT + 2, :], c_hi_lo), (spread[:, :], c_spread),
                (bias_in[0:1, :], b_out.rearrange("(a n) -> a n", a=1)),
                (bias_in[1:2, :], b_out.rearrange("(a n) -> a n", a=1)),
            ):
                act.dma_start(dst, src).then_inc(su_in, 16)
            for b in range(B):
                act.dma_start(o_tile[b * TOK:(b + 1) * TOK, 1, 0:CAD], ctx[b, KEYS:CTX, :]).then_inc(su_in, 16)
            act.wait_ge(vw2_ready, 1)
            for r, part in enumerate((vw2_h, vw2_l, vw2_h)):
                act.dma_start(vw2_all[r], part.bitcast(F32)).then_inc(vw2_out, 16)
            with act.Fori(0, B) as b:
                act.wait_ge(enc_full, b + 1)
                nc.scalar.activation(enc_t[:, :, :].rearrange("p c k -> p (c k)"), ps_t[:, 0, 0:CT * KEYS], copy).then_inc(enc_ready, 1)
                act.wait_ge(kv_full, b + 1)
                for half in range(2):
                    nc.scalar.activation(v_main[:, half * GRP:(half + 1) * GRP, 0:DH],
                                         ps_w[:, half, 0:HALF].rearrange("p (h d) -> p h d", h=GRP), copy)
                    tail = (ps_s[0:REM, 2, 0:HALF], ps_t[0:REM, 1, 0:HALF])[half]
                    last = nc.scalar.activation(v_tail[:, half * HALF:(half + 1) * HALF], tail, copy)
                last.then_inc(vals_ready, 1)
                def g_high_part(i):
                    act.wait_ge(gx_used, b * GX + (i + 1) * KT)
                    nc.scalar.activation(g[0:3 * HT, i * CHUNK:(i + 1) * CHUNK], g_banks[i % 2], copy).then_inc(g_high, 1)

                for m in range(GX):
                    i, kt = divmod(m, KT)
                    act.wait_ge(gx_turned, b * GX + m + 1)
                    if i:
                        act.wait_ge(gx_used, b * GX + m - KT + 1)
                    nc.scalar.activation(xt_h[:, kt, :], gx_banks[m % GX_BANKS], copy).then_inc(gx_high, 1)
                    if i and kt == GX_LAG:
                        g_high_part(i - 1)
                g_high_part(CHUNKS - 1)

                def copy_sums(h, k):
                    act.wait_ge(w_used, (b * HEADS + h + 1) * NST + 4)
                    nc.scalar.activation(hsu[0:VW, k, :], ps_s[0:VW, 2, 0:CAD], copy).then_inc(hsu_ready, 1)

                def head(h, k, first):
                    hh = b * HEADS + h
                    for st in range(NST):
                        if st == 1 and not first:
                            copy_sums(h - 1, 1 - k)
                        act.wait_ge(sc_full, START + hh * NST + st + 1)
                        act.wait_ge(w_used, hh * NST + st + 1)
                        nc.scalar.activation(caw[:, st % 4, :], ps_w[:, st % 2, 0:CAD], exp, scale=SCALE).then_inc(w_ready, 1)

                head(0, 0, True)
                head(1, 1, False)
                with act.Fori(1, HEADS // 2) as hp:
                    head(hp * 2, 0, False)
                    head(hp * 2 + 1, 1, False)
                copy_sums(HEADS - 1, 1)
                act.wait_ge(s2_ready, START + b + 1)
                nc.scalar.activation(p2[:, :, :], s2[:, :, :], exp, scale=SCALE).then_inc(e2_ready, 1)

                tile0 = b * SLOTS

                def high(dst, use):
                    act.wait_ge(t_full[bank_of(use)], filled(b, use))
                    nc.scalar.activation(dst, ps_t[:, bank_of(use), :], copy).then_inc(t_high, 1)

                def turned_weights(dst, src, use):
                    act.wait_ge(t_full[bank_of(use)], filled(b, use))
                    nc.scalar.activation(dst, src, copy).then_inc(t_free[bank_of(use)], 1)

                def weights(s):
                    if s:
                        use = ("p", s - 1, 1)
                        act.wait_ge(t_full[bank_of(use)], filled(b, use))
                    act.wait_ge(nmax_ready, tile0 + s + 1)
                    for h in range(HEADS):
                        bank, c = h // 3, h % 3
                        last = nc.scalar.activation(probs[:, h, :], ps_s[:, bank, c * KEYS:(c + 1) * KEYS], exp,
                                                    bias=neg_max[:, s % 2, h:h + 1], scale=SCALE)
                    last.then_inc(p_ready, 1)

                def store(s):
                    act.wait_ge(y_ready, START + tile0 + s + 1)
                    act.dma_start(out_rows[bass.ds(tile0 + s, 1)].rearrange("a p n -> p (a n)"),
                                  o_tile[:, s % 2, :]).then_inc(stored[s % 2], 16)

                for kt in range(KT):
                    high(xt_h[:, kt, :], ("x", 0, kt))
                for j in range(KT):
                    high(qt_h[:, j, :], ("q", 0, j))
                weights(0)
                for s in range(SLOTS):
                    c, t = divmod(s, ST)
                    if t == ST - 1 and c + 1 < CHUNKS:
                        for j in range(KT):
                            high(qt_h[:, j, :], ("q", c + 1, j))
                    use = ("p", s, 0)
                    turned_weights(probs_t[:, 0:GRP, :], ps_t[:, bank_of(use), :].rearrange("p (r s) -> p r s", r=GRP), use)
                    if s + 1 < SLOTS:
                        weights(s + 1)
                    use = ("p", s, 2)
                    turned_weights(probs_t[0:GRP * REM, HEADS:HEADS + 2, :],
                                   ps_t[0:GRP * REM, bank_of(use), 0:2 * P].rearrange("p (r s) -> p r s", r=2), use)
                    if s > 1:
                        store(s - 2)
                    if c + 1 < CHUNKS:
                        for kt in X_EARLY[t] + X_LATE[t]:
                            high(xt_h[:, kt, :], ("x", c + 1, kt))
                    for bank in range(2):
                        act.wait_ge(t_full[bank], filled(b, ("o", s, bank)))
                    nc.scalar.activation(ot_h[:, s % 2, :], ps_t_flat[:, 0:HID], copy).then_inc(ot_high, 1)
                store(SLOTS - 2)
                store(SLOTS - 1)
            for k in range(2):
                act.wait_ge(stored[k], START + 16 * B * SLOTS // 2)

        @block.vector
        def _(dve):
            v = nc.vector
            steps = Steps(dve, dve_setup, 0, 0)
            for started in (s2_ready, y_ready, ya_ready, z_free, hsu_ready, sc_full, *t_free, *stored):
                dve.sem_inc(started, START)
            dve.sem_inc(w_used, 4)
            v.memset(p2_rows[3 * HT:3 * HT + 2, :, :].bitcast(F32), 1.0)
            v.memset(v_main[:, :, DH:VW], 1.0)
            v.memset(m2[:, :, :, :], 0.0)
            steps.done(v.memset(v_rem[:, :, :, :], 0.0))
            dve.wait_ge(su_turned, 1)
            for j, src in enumerate((ps_t_flat, ps_s_flat, ps_w_flat)):
                v.tensor_copy(wq_t[j], src[:, 0:HID])
            n = CT * B * TOK + KT * TOK
            v.tensor_copy(small_t, ps_s[:, 2, 0:n]).then_inc(su_turned_ready, 1)
            dve.wait_ge(su_turned_ready, 1)
            v.tensor_copy(m2[:, :, :, HT:HT + 1], last_row[:, :].unsqueeze(1).unsqueeze(1).broadcast_to([VW, HEADS, B, 1]))
            for r in range(2):
                v.tensor_copy(v_rem[:, r, :, DH], rem_of[:, :])
            rows = slice(3 * HT, 3 * HT + 2)
            steps.done(v.tensor_copy(vw2_b[rows, :], bias_in))
            steps.done(v.tensor_tensor(bias_tmp, bias_in, vw2_b[rows, :], ALU.subtract))
            steps.done(v.tensor_scalar(bias_tmp, bias_tmp, hi_lo[rows, 1:2], None, ALU.mult))
            steps.done(v.scalar_tensor_tensor(bias_in, vw2_b[rows, :], hi_lo[rows, 0:1], bias_tmp, ALU.mult, ALU.add))
            v.tensor_copy(vw2_b[rows, :], bias_in)
            steps.done(v.tensor_copy(wq_h[:, :, :], stage_w))
            steps.done(v.tensor_tensor(wq_l[:, :, :], stage_w, wq_h[:, :, :], ALU.subtract))
            dve.wait_ge(kv2_full, 1)
            v.tensor_copy(wq_t[3], ps_t_flat[:, 0:HID])
            v.tensor_copy(wq_t[4], ps_s_flat[:, 0:HID])
            steps.done(v.tensor_copy(kv2_t.rearrange("p a j n -> p (a j n)"), ps_w[:, 0, 0:2 * KT * B * TOK]))
            for j in range(KT):
                mask = head_of[:, j, :].unsqueeze(1).unsqueeze(3).broadcast_to([P, B, HEADS, TOK])
                for a, dst in enumerate((k2_bd, v2_bd)):
                    src = kv2_t[:, a, j, :].rearrange("p (b t) -> p b t", b=B).unsqueeze(2).broadcast_to([P, B, HEADS, TOK])
                    last = v.tensor_tensor(dst[:, j, :].rearrange("p (b h t) -> p b h t", b=B, h=HEADS), src, mask, ALU.mult)
            last.then_inc(kv2_ready, 1)
            wg_src = wqca_t.unsqueeze(2).broadcast_to([P, KT, HEADS, TOK])
            wg_mask = head_of[:, :, :].unsqueeze(3).broadcast_to([P, KT, HEADS, TOK])
            steps.done(v.tensor_tensor(wg_full.rearrange("p k (h t) -> p k h t", h=HEADS), wg_src, wg_mask, ALU.mult))
            for r in range(3):
                last = v.tensor_copy(wg_h[:, :, r * HT:(r + 1) * HT], wg_full)
            steps.done(last)
            for r in range(3):
                last = v.tensor_tensor(wg_l[:, :, r * HT:(r + 1) * HT], wg_full, wg_h[:, :, 0:HT], ALU.subtract)
            dve.wait_ge(m2_rows_full, 1)
            for half in range(2):
                last = v.tensor_copy(m2_rows[:, half * HALF:(half + 1) * HALF], ps_s[:, half, 0:HALF])
            last.then_inc(m2_rows_ready, 1)
            dve.wait_ge(vw2_full, 1)
            halves = lambda a: a.rearrange("p (a n) -> p a n", a=2)
            steps.done(v.tensor_copy(halves(vw2_h), ps_t[:, 0:2, 0:HALF]))
            v.tensor_tensor(halves(vw2_l), ps_t[:, 0:2, 0:HALF], halves(vw2_h), ALU.subtract).then_inc(vw2_ready, 1)
            dve.wait_ge(m2_full, 1)
            for a in range(2):
                last = v.tensor_copy(m2[0:DH, a * 4:(a + 1) * 4, :, 0:HT],
                                     ps_w[0:DH, a, :].rearrange("p (h b n) -> p h b n", h=4, b=B))
            last.then_inc(m2_ready, 1)
            dve.wait_ge(su_wout_in, 16)
            steps.done(v.tensor_copy(wo_h[:, :, :], stage_w))
            v.tensor_tensor(wo_l[:, :, :], stage_w, wo_h[:, :, :], ALU.subtract).then_inc(wo_ready, 1)

            with dve.Fori(0, B) as b:
                dve.wait_ge(kv_full, b + 1)
                steps = Steps(dve, dve_batch, b, 1)
                v.memset(g[3 * HT:3 * HT + 1, :].bitcast(F32), 1.0)
                v.memset(xh[:, :, :, DH:VW], 1.0).then_inc(ones_set, 1)
                steps.done(v.tensor_copy(ca_all[:, :], ps_w[0:3 * HT, 2, 0:CAD]))
                steps.close()
                low_rows = slice(HT, 2 * HT)
                v.tensor_tensor(ca_all[low_rows, :], ps_w[low_rows, 2, 0:CAD], ca_all[low_rows, :], ALU.subtract).then_inc(ca_ready, 1)

                def k_psum(j):
                    return ps_s[:, j // 3, j % 3 * KEYS:(j % 3 + 1) * KEYS]

                def g_low_part(i):
                    dve.wait_ge(g_high, b * CHUNKS + i + 1)
                    low_rows, at = slice(2 * HT, 3 * HT), slice(i * CHUNK, (i + 1) * CHUNK)
                    v.tensor_tensor(g[low_rows, at], ps_w[low_rows, i % 2 * 2, :], g[low_rows, at], ALU.subtract).then_inc(g_ready, 1)

                for m in range(GX):
                    i, kt = divmod(m, KT)
                    dve.wait_ge(gx_high, b * GX + m + 1)
                    v.tensor_tensor(xt_l[:, kt, :], gx_banks[m % GX_BANKS], xt_h[:, kt, :], ALU.subtract).then_inc(gx_low, 1)
                    if m < len(PAIRS):
                        j, h = PAIRS[m]
                        v.tensor_scalar(keys_h[:, m, :], k_psum(j), head_of[:, j, h:h + 1], None, ALU.mult).then_inc(keys_high, 1)
                    if 1 <= m <= len(PAIRS):
                        j, h = PAIRS[m - 1]
                        dve.wait_ge(keys_high, b * len(PAIRS) + m)
                        last = v.scalar_tensor_tensor(keys_l[:, m - 1, :], k_psum(j), head_of[:, j, h:h + 1],
                                                      keys_h[:, m - 1, :], ALU.mult, ALU.subtract)
                        if m == len(PAIRS):
                            last.then_inc(keys_ready, 1)
                    if i and kt == GX_LAG:
                        g_low_part(i - 1)
                g_low_part(CHUNKS - 1)

                def set_head(h, k):
                    v.tensor_scalar(ca_head[0:3 * HT, k, :], ca_all[:, :],
                                    block_of[:, bass.ds(h, 1)] if not isinstance(h, int) else block_of[:, h:h + 1],
                                    None, ALU.mult).then_inc(head_set, 1)

                def maxima(h, k, adding=None):
                    first = (b * HEADS + h) * 2 * CT
                    for u in range(2 * CT):
                        if u == 3 and adding is not None:
                            add_head(adding)
                        dve.wait_ge(max_full, first + u + 1)
                        src = ps_t if u % 2 else ps_s
                        v.tensor_reduce(unit_max[:, k, u:u + 1], src[:, 0:2, :], mybir.AxisListType.XY, ALU.max).then_inc(max_free, 1)
                    dve.wait_ge(max_free, first + 2 * CT)
                    v.tensor_reduce(row_max[:, k, :], unit_max[:, k, :].rearrange("p (c a) -> p c a", a=2), AX_X, ALU.max).then_inc(rmax_ready, 1)
                    dve.wait_ge(rmax_t, b * HEADS + h + 1)
                    v.tensor_scalar(ca_head[3 * HT:3 * HT + 1, k, :], ps_w[0:1, 2, 0:CAD], -1.0, None, ALU.mult).then_inc(head_ready, 1)

                def add_head(h):
                    hh = b * HEADS + h
                    dve.wait_ge(z_full, hh + 1)
                    z = ps_w[0:WIN, 2, 0:CHUNKS * (HT + 1)].rearrange("p (w n) -> p w n", w=CHUNKS)
                    v.reciprocal(z_rec[:, :], z[:, :, HT]).then_inc(z_rec_ready, 1)
                    dve.wait_ge(z_rec_ready, hh + 1)
                    first = isinstance(h, int) and h == 0
                    v.tensor_tensor((s2 if first else z_norm)[:, :, :], z[:, :, 0:HT],
                                    z_rec[:, :].unsqueeze(2).broadcast_to([WIN, CHUNKS, HT]), ALU.mult).then_inc(z_free, 1)
                    dve.wait_ge(z_free, START + hh + 1)
                    if not first:
                        if not isinstance(h, int) or h > 1:
                            dve.wait_ge(s2_added, b * (HEADS - 1) + h - 1)
                        v.tensor_tensor(s2[:, :, :], s2[:, :, :], z_norm[:, :, :], ALU.add).then_inc(s2_added, 1)

                def head(h, k, first):
                    dve.wait_ge(sc_full, START + (b * HEADS + h) * NST)
                    set_head(h + 1, 1 - k)
                    maxima(h + 1, 1 - k, None if first else h - 1)

                set_head(0, 0)
                maxima(0, 0)
                head(0, 0, True)
                head(1, 1, False)
                with dve.Fori(1, HEADS // 2 - 1) as hp:
                    head(hp * 2, 0, False)
                    head(hp * 2 + 1, 1, False)
                head(HEADS - 2, 0, False)
                add_head(HEADS - 2)
                add_head(HEADS - 1)
                dve.wait_ge(s2_added, (b + 1) * (HEADS - 1))
                steps = Steps(dve, dve_p2, b, 4)
                by_head = lambda a: a[:, :, :].rearrange("p w (h t) -> p (w h) t", t=TOK)
                spread_t = s2_max[:, :].unsqueeze(2).broadcast_to([WIN, CHUNKS * HEADS, TOK])
                steps.done(v.tensor_reduce(s2_max[:, :], by_head(s2), AX_X, ALU.max))
                v.tensor_tensor(by_head(s2), by_head(s2), spread_t, ALU.subtract).then_inc(s2_ready, 1)
                dve.wait_ge(e2_ready, b + 1)
                steps.done(v.tensor_reduce(s2_max[:, :], by_head(p2), AX_X, ALU.add))
                steps.done(v.reciprocal(s2_max[:, :], s2_max[:, :]))
                steps.done(v.tensor_tensor(by_head(p2), by_head(p2), spread_t, ALU.mult))
                for r in range(3):
                    last = v.tensor_copy(p2_rep[:, :, r, :], p2[:, :, :])
                last.then_inc(p2_ready, 1)
                steps.close()

                tile0 = b * SLOTS
                steps = Steps(dve, dve_tile, b, CHUNKS + 3 * SLOTS)
                dve.wait_ge(p2_ready, b + 1)

                def low(dst, high_part, use):
                    dve.wait_ge(t_high, b * T_HIGHS + T_HIGH[use] + 1)
                    v.tensor_tensor(dst, ps_t[:, bank_of(use), :], high_part, ALU.subtract).then_inc(t_free[bank_of(use)], 1)

                def pick_window(c):
                    v.tensor_copy(p2_chunk[:, :], p2_rep[:, c, :, :].rearrange("p r n -> p (r n)")).then_inc(p2c_ready, 1)

                def picked(c):
                    use = ("gather", c)
                    dve.wait_ge(t_full[bank_of(use)], filled(b, use))
                    steps.done(v.tensor_copy(p2_rows[0:3 * HT, c % 2, :], ps_t[0:3 * HT, bank_of(use), :]))
                    low_rows = slice(2 * HT, 3 * HT)
                    v.tensor_tensor(p2_rows[low_rows, c % 2, :], ps_t[low_rows, bank_of(use), :], p2_rows[low_rows, c % 2, :],
                                    ALU.subtract).then_inc(t_free[bank_of(use)], 1)

                def maximum(s):
                    dve.wait_ge(s_full, tile0 + s + 1)
                    v.tensor_reduce(neg_max[:, s % 2, 0:6].rearrange("p (a h) -> p a h", a=2),
                                    ps_s[:, 0:2, 0:3 * KEYS].rearrange("p a (h k) -> p a h k", h=3), AX_X, ALU.max)
                    steps.done(v.tensor_reduce(neg_max[:, s % 2, 6:8], ps_s[:, 2, 0:2 * KEYS].rearrange("p (h k) -> p h k", h=2),
                                               AX_X, ALU.max))
                    v.tensor_scalar(neg_max[:, s % 2, :], neg_max[:, s % 2, :], -SCALE, None, ALU.mult).then_inc(nmax_ready, 1)

                def remaining(s):
                    dve.wait_ge(p_ready, tile0 + s + 1)
                    v.tensor_copy(probs_rem[:, :, :], probs[:, :, P:KEYS]).then_inc(rem_ready, 1)

                def turned_weights(s):
                    use = ("p", s, 1)
                    dve.wait_ge(t_full[bank_of(use)], filled(b, use))
                    v.tensor_copy(probs_t[:, GRP:HEADS, :],
                                  ps_t[:, bank_of(use), :].rearrange("p (r s) -> p r s", r=GRP)).then_inc(t_free[bank_of(use)], 1)

                def normalise(s):
                    for r in range(2):
                        dve.wait_ge(ov_full, (tile0 + s) * 2 + r + 1)
                        o = ps_w[:, 2 if r == 0 else 0, 0:GRP * VW].rearrange("p (q v) -> p q v", q=GRP)
                        steps.done(v.reciprocal(o_rec[:, r * GRP:(r + 1) * GRP], o[:, :, DH]))
                        last = v.tensor_tensor(o_norm[:, r * HALF:(r + 1) * HALF].rearrange("p (q d) -> p q d", q=GRP),
                                               o[:, :, 0:DH],
                                               o_rec[:, r * GRP:(r + 1) * GRP].unsqueeze(2).broadcast_to([P, GRP, DH]), ALU.mult)
                    last.then_inc(on_ready, 1)

                def add_rows(s, half):
                    c, t = divmod(s, ST)
                    if half == 0:
                        dve.wait_ge(stored[s % 2], START + 16 * (b * (SLOTS // 2) + s // 2))
                    dve.wait_ge(y_full, (tile0 + s) * 2 + half + 1)
                    cols = slice(half * HALF, (half + 1) * HALF)
                    v.tensor_tensor(o_tile[:, s % 2, cols], ps_w[:, half, 0:HALF], xc[:, c % 2 * ST + t, cols],
                                    ALU.add).then_inc((ya_ready, y_ready)[half], 1)

                pick_window(0)
                for kt in range(KT):
                    low(xt_l[:, kt, :], xt_h[:, kt, :], ("x", 0, kt))
                for j in range(KT):
                    low(qt_l[:, j, :], qt_h[:, j, :], ("q", 0, j))
                picked(0)
                maximum(0)
                for s in range(SLOTS):
                    c, t = divmod(s, ST)
                    remaining(s)
                    if t == ST - 1 and c + 1 < CHUNKS:
                        for j in range(KT):
                            low(qt_l[:, j, :], qt_h[:, j, :], ("q", c + 1, j))
                    if s + 1 < SLOTS:
                        maximum(s + 1)
                    turned_weights(s)
                    if s:
                        add_rows(s - 1, 0)
                    if c + 1 < CHUNKS:
                        for kt in X_EARLY[t]:
                            low(xt_l[:, kt, :], xt_h[:, kt, :], ("x", c + 1, kt))
                        if t == GATHER_AT:
                            pick_window(c + 1)
                    normalise(s)
                    if c + 1 < CHUNKS:
                        for kt in X_LATE[t]:
                            low(xt_l[:, kt, :], xt_h[:, kt, :], ("x", c + 1, kt))
                        if t == GATHER_AT:
                            picked(c + 1)
                    dve.wait_ge(ot_high, tile0 + s + 1)
                    v.tensor_tensor(ot_l[:, s % 2, :], ps_t_flat[:, 0:HID], ot_h[:, s % 2, :], ALU.subtract).then_inc(ot_low, 1)
                    if s:
                        add_rows(s - 1, 1)
                add_rows(SLOTS - 1, 0)
                add_rows(SLOTS - 1, 1)
                steps.close()


_INS = ["x", "ctx_768", "L0_xattn_Wq", "L0_xattn_Wk", "L0_xattn_Wv", "L0_xattn_Wq_ca", "L0_xattn_Wk_ca",
        "L0_xattn_Wv_ca", "L0_xattn_Wout", "L0_xattn_b_out"]
_CONSTS = ["ident", "head_of", "block_of", "pick", "rem_of", "last_row", "hi_lo", "spread"]


def kernel(**inputs):
    import concourse.bacc as _bacc
    from concourse.bass_utils import run_bass_kernel_spmd as _run

    nc = _bacc.Bacc("TRN2", target_bir_lowering=False, num_devices=1)
    consts = constants()
    arrays, args = {}, []
    for name, a in [(n, inputs[n]) for n in _INS] + [(n, consts[n]) for n in _CONSTS]:
        a = np.ascontiguousarray(a)
        arrays[f"in_{name}_dram"] = a
        args.append(nc.dram_tensor(f"in_{name}_dram", a.shape, mybir.dt.from_np(a.dtype), kind="ExternalInput").ap())
    out = nc.dram_tensor("out_dram", (B, S, HID), F32, kind="ExternalOutput").ap()
    cross_attention(nc, *args, out)
    r = _run(nc, [arrays], core_ids=[0])
    return r.results[0]["out_dram"]
```
